# Optimizing a Trainium2 kernel written in Bass

```python
import numpy as np
import jax
import jax.numpy as jnp

def _softmax(x, axis=-1):
    return jax.nn.softmax(x, axis=axis)

def _gelu(x):
    return jax.nn.gelu(x, approximate=True)

def _silu(x):
    return jax.nn.silu(x)

def _sigmoid(x):
    return jax.nn.sigmoid(x)

def _layernorm(x, axis=-1, eps=1e-05):
    m = jnp.mean(x, axis=axis, keepdims=True)
    v = jnp.var(x, axis=axis, keepdims=True)
    return (x - m) / jnp.sqrt(v + eps)

def _scatter_add(tgt, idx, src, axis=0):
    return tgt.at[idx].add(src)

def _segment_sum(src, seg, n):
    return jax.ops.segment_sum(src, seg, n)
kernel_name = 'mk_rec_standalone_d1_rec_r8_69416d'

def setup_inputs(seed: int=0):
    np.random.seed(seed)
    _w = jnp.asarray

    def _rec_inputs():
        import jax
        import jax.numpy as jnp
        _rk = jax.random.key(seed)
        r_dense = -0.00338568 + 1.0005 * jax.random.normal(jax.random.fold_in(_rk, 1), (2048, 13), jnp.float32)
        r_s0 = jax.random.randint(jax.random.fold_in(_rk, 2), (2048,), 13, 999973, jnp.int32)
        r_s1 = jax.random.randint(jax.random.fold_in(_rk, 3), (2048,), 17, 199980, jnp.int32)
        r_s2 = jax.random.randint(jax.random.fold_in(_rk, 4), (2048,), 9, 99996, jnp.int32)
        r_s3 = jax.random.randint(jax.random.fold_in(_rk, 5), (2048,), 0, 375, jnp.int32)
        r_s4 = jax.random.randint(jax.random.fold_in(_rk, 6), (2048,), 0, 375, jnp.int32)
        r_s5 = jax.random.randint(jax.random.fold_in(_rk, 7), (2048,), 0, 1000, jnp.int32)
        r_s6 = jax.random.randint(jax.random.fold_in(_rk, 8), (2048,), 0, 500, jnp.int32)
        r_s7 = jax.random.randint(jax.random.fold_in(_rk, 9), (2048,), 0, 100, jnp.int32)
        return (r_dense, r_s0, r_s1, r_s2, r_s3, r_s4, r_s5, r_s6, r_s7)
    r_dense, r_s0, r_s1, r_s2, r_s3, r_s4, r_s5, r_s6, r_s7 = _rec_inputs()

    def _L0_rec_setup():
        import jax, jax.numpy as jnp
        import numpy as np
        B = 2048
        D = 64
        ND = 13
        VOCABS = [125000, 25000, 12500, 375, 375, 1000, 500, 100]
        H_IN = (len(VOCABS) + 1) * D
        key = jax.random.key(seed)
        ks = jax.random.split(key, 40)
        inp = {'dense': jax.random.normal(ks[0], (B, ND), jnp.float32)}
        for i, v in enumerate(VOCABS):
            inp[f's{i}'] = jax.random.randint(ks[1 + i], (B,), 0, v)
            inp[f'E{i}'] = jax.random.normal(ks[9 + i], (v, D), jnp.float32) * 0.01
            inp[f'w{i}'] = jax.random.normal(ks[17 + i], (v, 1), jnp.float32) * 0.01
        inp['wc0'] = jax.random.normal(ks[25], (VOCABS[3] * VOCABS[4], 1), jnp.float32) * 0.01
        inp['wc1'] = jax.random.normal(ks[26], (VOCABS[5] * VOCABS[6], 1), jnp.float32) * 0.01
        inp['Wd_deep'] = jax.random.normal(ks[27], (ND, D), jnp.float32) * 0.05
        inp['Wd_wide'] = jax.random.normal(ks[28], (ND, 1), jnp.float32) * 0.05
        inp['W1'] = jax.random.normal(ks[29], (H_IN, 512), jnp.float32) * 0.02
        inp['W2'] = jax.random.normal(ks[30], (512, 256), jnp.float32) * 0.02
        inp['W3'] = jax.random.normal(ks[31], (256, 1), jnp.float32) * 0.02
        inp['bias'] = jnp.zeros((1, 1), jnp.float32)
        return inp
    _L0_rec_all = _L0_rec_setup()
    _L0_rec_in = {k: v for k, v in _L0_rec_all.items() if k in ('E0', 'E1', 'E2', 'E3', 'E4', 'E5', 'E6', 'E7', 'w0', 'w1', 'w2', 'w3', 'w4', 'w5', 'w6', 'w7', 'wc0', 'wc1', 'Wd_deep', 'Wd_wide', 'W1', 'W2', 'W3', 'bias')}
    del _L0_rec_all
    return {'r_dense': r_dense, 'r_s0': r_s0, 'r_s1': r_s1, 'r_s2': r_s2, 'r_s3': r_s3, 'r_s4': r_s4, 'r_s5': r_s5, 'r_s6': r_s6, 'r_s7': r_s7, 'L0_rec_E0': _L0_rec_in['E0'], 'L0_rec_E1': _L0_rec_in['E1'], 'L0_rec_E2': _L0_rec_in['E2'], 'L0_rec_E3': _L0_rec_in['E3'], 'L0_rec_E4': _L0_rec_in['E4'], 'L0_rec_E5': _L0_rec_in['E5'], 'L0_rec_E6': _L0_rec_in['E6'], 'L0_rec_E7': _L0_rec_in['E7'], 'L0_rec_w0': _L0_rec_in['w0'], 'L0_rec_w1': _L0_rec_in['w1'], 'L0_rec_w2': _L0_rec_in['w2'], 'L0_rec_w3': _L0_rec_in['w3'], 'L0_rec_w4': _L0_rec_in['w4'], 'L0_rec_w5': _L0_rec_in['w5'], 'L0_rec_w6': _L0_rec_in['w6'], 'L0_rec_w7': _L0_rec_in['w7'], 'L0_rec_wc0': _L0_rec_in['wc0'], 'L0_rec_wc1': _L0_rec_in['wc1'], 'L0_rec_Wd_deep': _L0_rec_in['Wd_deep'], 'L0_rec_Wd_wide': _L0_rec_in['Wd_wide'], 'L0_rec_W1': _L0_rec_in['W1'], 'L0_rec_W2': _L0_rec_in['W2'], 'L0_rec_W3': _L0_rec_in['W3'], 'L0_rec_bias': _L0_rec_in['bias']}

def reference(r_dense, r_s0, r_s1, r_s2, r_s3, r_s4, r_s5, r_s6, r_s7, L0_rec_E0, L0_rec_E1, L0_rec_E2, L0_rec_E3, L0_rec_E4, L0_rec_E5, L0_rec_E6, L0_rec_E7, L0_rec_w0, L0_rec_w1, L0_rec_w2, L0_rec_w3, L0_rec_w4, L0_rec_w5, L0_rec_w6, L0_rec_w7, L0_rec_wc0, L0_rec_wc1, L0_rec_Wd_deep, L0_rec_Wd_wide, L0_rec_W1, L0_rec_W2, L0_rec_W3, L0_rec_bias):
    import jax
    import jax.numpy as jnp

    def _L0_rec_ref(dense, s0, s1, s2, s3, s4, s5, s6, s7, E0, E1, E2, E3, E4, E5, E6, E7, w0, w1, w2, w3, w4, w5, w6, w7, wc0, wc1, Wd_deep, Wd_wide, W1, W2, W3, bias):
        import jax, jax.numpy as jnp
        import numpy as np
        B = 2048
        D = 64
        ND = 13
        VOCABS = [125000, 25000, 12500, 375, 375, 1000, 500, 100]
        H_IN = (len(VOCABS) + 1) * D
        S = [s0, s1, s2, s3, s4, s5, s6, s7]
        E = [E0, E1, E2, E3, E4, E5, E6, E7]
        w = [w0, w1, w2, w3, w4, w5, w6, w7]
        wide = dense @ Wd_wide
        for si, wi in zip(S, w):
            wide = wide + wi[si]
        wide = wide + wc0[S[3] * VOCABS[4] + S[4]]
        wide = wide + wc1[S[5] * VOCABS[6] + S[6]]
        deep_in = jnp.concatenate([dense @ Wd_deep] + [Ei[si] for Ei, si in zip(E, S)], axis=1)
        h = jax.nn.relu(deep_in @ W1)
        h = jax.nn.relu(h @ W2)
        deep = h @ W3
        return bias + deep + wide
    y = _L0_rec_ref(r_dense, r_s0, r_s1, r_s2, r_s3, r_s4, r_s5, r_s6, r_s7, L0_rec_E0, L0_rec_E1, L0_rec_E2, L0_rec_E3, L0_rec_E4, L0_rec_E5, L0_rec_E6, L0_rec_E7, L0_rec_w0, L0_rec_w1, L0_rec_w2, L0_rec_w3, L0_rec_w4, L0_rec_w5, L0_rec_w6, L0_rec_w7, L0_rec_wc0, L0_rec_wc1, L0_rec_Wd_deep, L0_rec_Wd_wide, L0_rec_W1, L0_rec_W2, L0_rec_W3, L0_rec_bias)
    return y

_drawn_inputs = setup_inputs


def setup_inputs(seed=0):
    import zlib

    import numpy as np

    out = dict(_drawn_inputs(seed))
    spreads = {}
    factors = {'L0_rec_E0': 8.0,
     'L0_rec_E1': 8.0,
     'L0_rec_E2': 8.0,
     'L0_rec_E3': 8.0,
     'L0_rec_E4': 8.0,
     'L0_rec_E5': 8.0,
     'L0_rec_E6': 8.0,
     'L0_rec_E7': 8.0,
     'L0_rec_Wd_deep': 7.114,
     'L0_rec_W1': 5.509,
     'L0_rec_W2': 5.635,
     'L0_rec_W3': 5.254,
     'L0_rec_w0': 22.994,
     'L0_rec_w1': 7.08,
     'L0_rec_w2': 8.0,
     'L0_rec_w3': 8.0,
     'L0_rec_w4': 8.0,
     'L0_rec_w5': 8.0,
     'L0_rec_w6': 8.0,
     'L0_rec_w7': 8.0,
     'L0_rec_wc0': 8.0,
     'L0_rec_wc1': 8.0}
    for name, (base, spread) in spreads.items():
        noise = np.random.default_rng([zlib.crc32(name.encode()), seed]).standard_normal(out[name].shape)
        drawn = base * np.exp(spread * noise) if base else spread * noise
        out[name] = jnp.asarray(drawn.astype(out[name].dtype))
    for name, factor in factors.items():
        out[name] = (out[name] * factor).astype(out[name].dtype)
    return out
```

```python
import numpy as np

import concourse.bass as bass
from concourse import mybir
from contextlib import ExitStack

P = 128
BATCH = 2048
D = 64
ND = 13
VOCABS = [125000, 25000, 12500, 375, 375, 1000, 500, 100]
H1, H2 = 512, 256

GATHERED = [0, 1, 2]
LOOKED_UP = [3, 4, 5, 6, 7]
FIELDS = GATHERED + LOOKED_UP
NG, NL, NF = len(GATHERED), len(LOOKED_UP), len(FIELDS)
ROW = D + 1
CROSSES = [(3, 4), (5, 6)]
NX = len(CROSSES)
SPLIT = 3

TILES = BATCH // P
BLOCK = 512
BT = BLOCK // P
BLOCKS = BATCH // BLOCK
PAIRS = BLOCKS // 2
PT = 2 * BT

CHUNKS = [-(-VOCABS[f] // P) for f in LOOKED_UP]
CHUNK0 = [sum(CHUNKS[:i]) for i in range(NL)]
NCH = sum(CHUNKS)
FGROUPS = [list(range(i, min(i + 2, NL))) for i in range(0, NL, 2)]
NGR = len(FGROUPS)
KB = NF * D // P
M1, M2 = H1 // P, H2 // P
NROWS = SPLIT * SPLIT * ND


def program(nc, index, dense_t, big, small, wc, wd_deep_t, wd_wide, w1, w2, w3, bias, out):
    f32, bf16, f16, i32 = mybir.dt.float32, mybir.dt.bfloat16, mybir.dt.float16, mybir.dt.int32
    ALU, ACT, AX = mybir.AluOpType, mybir.ActivationFunctionType, mybir.AxisListType
    scratch = nc.dram_tensor("index_rows", (PAIRS, NL * PT * P), f16, kind="Internal").ap()

    with ExitStack() as ctx:
        def sb(name, shape, dt):
            return ctx.enter_context(nc.sbuf_tensor(name, shape, dt))

        def pb(name, shape):
            return ctx.enter_context(nc.psum_tensor(name, shape, f32))

        def sem(name):
            return ctx.enter_context(nc.semaphore(name))

        idx_raw = sb("idx_raw", [P, NF, TILES], i32)
        idx_f = sb("idx_f", [P, NF + NX, TILES], f32)
        idx_wrap = sb("idx_wrap", [P, NF + NX, TILES], f32)
        idx_sum = sb("idx_sum", [P, NF + NX, TILES], f32)
        vocab = sb("vocab", [P, NF + NX, TILES], f32)
        vocab_last = sb("vocab_last", [P, NF + NX, TILES], f32)
        idx_gather = sb("idx_gather", [P, NG, TILES], i32)
        idx_cross = sb("idx_cross", [P, NX, TILES], i32)
        idx_look = sb("idx_look", [P, PAIRS, NL, PT], f32)
        idx_rows = sb("idx_rows", [PAIRS * NL * PT, P], f16)
        idx_bc = sb("idx_bc", [P, PAIRS, NL, PT * P], f16)
        ident0 = sb("ident0", [P, P], f32)
        ident = sb("ident", [P, P], f32)
        row_id = sb("row_id", [P, max(CHUNKS)], f32)
        table = sb("table", [P, NCH, ROW], f32)
        table_rest = sb("table_rest", [P, NCH, ROW], f32)
        table_parts = sb("table_parts", [P, NCH, SPLIT, ROW], bf16)
        onehot = [sb(f"onehot{h}", [P, NCH, BLOCK], bf16) for h in range(2)]
        dense_sb = sb("dense_sb", [ND, BATCH], f32)
        dense_rest = sb("dense_rest", [ND, BATCH], f32)
        dense_parts = sb("dense_parts", [ND, SPLIT, BATCH], bf16)
        dense_stack = sb("dense_stack", [NROWS, BATCH], bf16)
        wd_sb = sb("wd_sb", [D, ND], f32)
        w1d_sb = sb("w1d_sb", [D, H1], f32)
        wdense = sb("wdense", [ND, H1 + 1], f32)
        wdense_rest = sb("wdense_rest", [ND, H1 + 1], f32)
        wdense_parts = sb("wdense_parts", [ND, SPLIT, H1 + 1], bf16)
        wdense_stack = sb("wdense_stack", [NROWS, H1 + 1], bf16)
        w1_sb = sb("w1_sb", [P, KB, H1], f32)
        w2_sb = sb("w2_sb", [P, M1, H2], f32)
        w3_sb = sb("w3_sb", [P, M2], f32)
        bias_sb = sb("bias_sb", [P, 1], f32)
        x = [sb(f"x{h}", [P, BT, NF * ROW], f32) for h in range(2)]
        xt = [sb(f"xt{h}", [P, KB, BLOCK], f32) for h in range(2)]
        h1 = [sb(f"h1_{h}", [P, M1, BLOCK], f32) for h in range(2)]
        h2 = [sb(f"h2_{h}", [P, M2, BLOCK], f32) for h in range(2)]
        wide = sb("wide", [P, TILES], f32)
        cross = sb("cross", [P, NX, TILES], f32)
        cross_sum = sb("cross_sum", [P, TILES], f32)
        wide_sum = sb("wide_sum", [P, TILES], f32)
        result = sb("result", [P, TILES], f32)

        look_ps = [pb(f"look_ps{k}", [P, len(FGROUPS[k]), SPLIT, ROW]) for k in range(NGR)]
        tr_ps = [pb(f"tr_ps{k}", [P, BLOCK]) for k in range(2)]
        mm_ps = [pb(f"mm_ps{k}", [P, BLOCK]) for k in range(2)]
        deep_ps = pb("deep_ps", [P, TILES])

        index_loaded = sem("index_loaded")
        table_loaded = sem("table_loaded")
        dense_loaded = sem("dense_loaded")
        wd_loaded = sem("wd_loaded")
        wide_weight_loaded = sem("wide_weight_loaded")
        w1_loaded = sem("w1_loaded")
        w23_loaded = sem("w23_loaded")
        bias_loaded = sem("bias_loaded")
        ident_zeroed = sem("ident_zeroed")
        consts_ready = sem("consts_ready")
        vocab_ready = sem("vocab_ready")
        index_ready = sem("index_ready")
        index_turned = sem("index_turned")
        index_rows_ready = sem("index_rows_ready")
        scratch_written = sem("scratch_written")
        index_spread = [sem(f"index_spread{j}") for j in range(PAIRS)]
        part_rounded = sem("part_rounded")
        rest_ready = sem("rest_ready")
        table_part_ready = sem("table_part_ready")
        wdense_done = sem("wdense_done")
        wdense_copied = sem("wdense_copied")
        wdense_part_ready = sem("wdense_part_ready")
        dense_part_ready = sem("dense_part_ready")
        dense_stacked = sem("dense_stacked")
        rows_gathered = [sem(f"rows_gathered{h}") for h in range(2)]
        cross_gathered = sem("cross_gathered")
        onehot_ready = sem("onehot_ready")
        looked_up = [sem(f"looked_up{h}") for h in range(2)]
        looked_up_summed = sem("looked_up_summed")
        turned = [sem(f"turned{h}") for h in range(2)]
        x_summed = [sem(f"x_summed{h}") for h in range(2)]
        turned_copied = sem("turned_copied")
        layer1_done = [sem(f"layer1_done{h}") for h in range(2)]
        layer2_done = [sem(f"layer2_done{h}") for h in range(2)]
        layer_copied = sem("layer_copied")
        deep_done = [sem(f"deep_done{h}") for h in range(2)]
        vector_step = sem("vector_step")
        result_ready = sem("result_ready")
        result_stored = sem("result_stored")

        L1_TURN = [0, M1 + M2]
        L2_TURN = [M1, 2 * M1 + M2]
        TURNS = 2 * (M1 + M2)
        CHUNK_END = [CHUNK0[g[-1]] + CHUNKS[g[-1]] for g in FGROUPS]

        splits = [
            (table[:], table_rest[:], [table_parts[:, :, i, :] for i in range(SPLIT)], table_part_ready),
            (dense_sb[:], dense_rest[:], [dense_parts[:, i, :] for i in range(SPLIT)], dense_part_ready),
            (wdense[:], wdense_rest[:], [wdense_parts[:, i, :] for i in range(SPLIT)], wdense_part_ready),
        ]

        block = ctx.enter_context(nc.Block())

        @block.sync
        def _(sp):
            sp.dma_start(idx_raw[:], index).then_inc(index_loaded, 16)
            sp.dma_start(table[:], small).then_inc(table_loaded, 16)
            sp.dma_start(wd_sb[:], wd_deep_t).then_inc(wd_loaded, 16)
            sp.dma_start(w1d_sb[:], w1[0:D, :]).then_inc(wd_loaded, 16)
            sp.dma_start(wdense[:, H1:H1 + 1], wd_wide).then_inc(wide_weight_loaded, 16)
            sp.dma_start(dense_sb[:], dense_t).then_inc(dense_loaded, 16)
            sp.wait_ge(index_rows_ready, 1)
            sp.dma_start(scratch.rearrange("j (r p) -> (j r) p", p=P), idx_rows[:]).then_inc(scratch_written, 16)
            sp.wait_ge(scratch_written, 16)
            for j in range(PAIRS):
                sp.dma_start(idx_bc[:, j].rearrange("p f n -> p (f n)"),
                             scratch[j:j + 1, :].to_broadcast([P, NL * PT * P])).then_inc(index_spread[j], 16)
            for f in FIELDS:
                k = FIELDS.index(f)
                sp.dma_start(w1_sb[(k % 2) * D:(k % 2 + 1) * D, k // 2, :],
                             w1[(1 + f) * D:(2 + f) * D, :]).then_inc(w1_loaded, 16)
            sp.dma_start(w2_sb[:], w2.rearrange("(k p) n -> p k n", p=P)).then_inc(w23_loaded, 16)
            sp.dma_start(w3_sb[:], w3.rearrange("p k -> p k")).then_inc(w23_loaded, 16)
            sp.dma_start(bias_sb[:], bias.to_broadcast([P, 1])).then_inc(bias_loaded, 16)
            sp.wait_ge(dense_part_ready, 1)
            sp.wait_ge(wdense_part_ready, 1)
            for a in range(SPLIT):
                for b in range(SPLIT):
                    r = (a * SPLIT + b) * ND
                    sp.dma_start(dense_stack[r:r + ND, :], dense_parts[:, a, :]).then_inc(dense_stacked, 16)
                    sp.dma_start(wdense_stack[r:r + ND, :], wdense_parts[:, b, :]).then_inc(dense_stacked, 16)
            sp.wait_ge(result_ready, 1)
            sp.dma_start(out, result[:]).then_inc(result_stored, 16)
            sp.wait_ge(result_stored, 16)

        @block.gpsimd
        def _(pool):
            nc.gpsimd.memset(ident0[:], 0.0).then_inc(ident_zeroed, 1)
            nc.gpsimd.iota(row_id[:], pattern=[[P, max(CHUNKS)]], base=0, channel_multiplier=1,
                           allow_small_or_imprecise_dtypes=True).then_inc(consts_ready, 1)
            pool.wait_ge(ident_zeroed, 1)
            nc.gpsimd.affine_select(out=ident[:], in_=ident0[:], compare_op=ALU.not_equal, fill=1.0, base=0,
                                    pattern=[[-1, P]], channel_multiplier=1).then_inc(consts_ready, 1)
            pool.wait_ge(index_ready, 1)

            def gather_rows(b):
                h = b % 2
                for s in range(BT):
                    for g in range(NG):
                        t = b * BT + s
                        nc.gpsimd.indirect_dma_start(
                            out=x[h][:, s, g * ROW:(g + 1) * ROW], out_offset=None, in_=big[g],
                            in_offset=bass.IndirectOffsetOnAxis(ap=idx_gather[:, g, t:t + 1], axis=0),
                        ).then_inc(rows_gathered[h], 16)

            for b in range(2):
                gather_rows(b)
            for c in range(NX):
                for t in range(TILES):
                    nc.gpsimd.indirect_dma_start(
                        out=cross[:, c, t:t + 1], out_offset=None, in_=wc[c],
                        in_offset=bass.IndirectOffsetOnAxis(ap=idx_cross[:, c, t:t + 1], axis=0),
                    ).then_inc(cross_gathered, 16)
            for b in range(2, BLOCKS):
                pool.wait_ge(turned[b % 2], b // 2 * KB)
                pool.wait_ge(x_summed[b % 2], b // 2)
                gather_rows(b)

        @block.scalar
        def _(act):
            act.wait_ge(index_turned, 1)
            nc.scalar.copy(idx_rows[:], tr_ps[0][0:PAIRS * NL * PT, 0:P]).then_inc(index_rows_ready, 1)
            act.wait_ge(wdense_done, 1)
            nc.scalar.copy(wdense[:, 0:H1], mm_ps[0][0:ND, :]).then_inc(wdense_copied, 1)
            for n, (src, rest, parts, _) in enumerate(splits):
                if n == 0:
                    act.wait_ge(table_loaded, 16)
                if n == 1:
                    act.wait_ge(dense_loaded, 16)
                if n == 2:
                    act.wait_ge(wdense_copied, 1)
                    act.wait_ge(wide_weight_loaded, 16)
                nc.scalar.copy(parts[0], src).then_inc(part_rounded, 1)
                act.wait_ge(rest_ready, n + 1)
                nc.scalar.copy(parts[1], rest).then_inc(part_rounded, 1)

            def copy_turned(j, h, g):
                n = h * KB + g
                act.wait_ge(turned[h], j * KB + g + 1)
                nc.scalar.copy(xt[h][:, g, :], tr_ps[n % 2][:]).then_inc(turned_copied, 1)

            def relu(turn, dst):
                nc.scalar.activation(dst, mm_ps[turn % 2][:], ACT.Relu).then_inc(layer_copied, 1)

            def relu1(j, h, m):
                act.wait_ge(layer1_done[h], j * M1 + m + 1)
                relu(L1_TURN[h] + m, h1[h][:, m, :])

            def relu2(j, h, n):
                act.wait_ge(layer2_done[h], j * M2 + n + 1)
                relu(L2_TURN[h] + n, h2[h][:, n, :])

            with act.Fori(0, PAIRS) as j:
                for g in range(KB):
                    copy_turned(j, 0, g)
                for m in range(M1):
                    relu1(j, 0, m)
                    copy_turned(j, 1, m)
                for n in range(M2):
                    relu2(j, 0, n)
                for m in range(M1):
                    relu1(j, 1, m)
                for n in range(M2):
                    relu2(j, 1, n)

        @block.vector
        def _(dve):
            steps = [0]

            def step(ins):
                steps[0] += 1
                ins.then_inc(vector_step, 1)
                dve.wait_ge(vector_step, steps[0])

            sizes = [VOCABS[f] for f in FIELDS] + [VOCABS[a] * VOCABS[b] for a, b in CROSSES]
            for k, v in enumerate(sizes):
                nc.vector.memset(vocab[:, k, :], float(v)).then_inc(vocab_ready, 1)
                nc.vector.memset(vocab_last[:, k, :], float(v - 1)).then_inc(vocab_ready, 1)
            dve.wait_ge(index_loaded, 16)
            step(nc.vector.tensor_copy(idx_f[:, 0:NF, :], idx_raw[:]))
            for c, (a, b) in enumerate(CROSSES):
                step(nc.vector.scalar_tensor_tensor(
                    out=idx_f[:, NF + c, :], in0=idx_f[:, FIELDS.index(a), :], scalar=float(VOCABS[b]),
                    in1=idx_f[:, FIELDS.index(b), :], op0=ALU.mult, op1=ALU.add))
            dve.wait_ge(vocab_ready, 2 * len(sizes))
            step(nc.vector.scalar_tensor_tensor(out=idx_wrap[:], in0=idx_f[:], scalar=0.0, in1=vocab[:],
                                                op0=ALU.is_lt, op1=ALU.mult))
            step(nc.vector.tensor_tensor(idx_sum[:], idx_wrap[:], idx_f[:], ALU.add))

            def clip(dst, lo, hi):
                return nc.vector.scalar_tensor_tensor(out=dst, in0=idx_sum[:, lo:hi], scalar=0.0,
                                                      in1=vocab_last[:, lo:hi], op0=ALU.max, op1=ALU.min)

            clip(idx_gather[:], 0, NG)
            for j in range(PAIRS):
                nc.vector.scalar_tensor_tensor(
                    out=idx_look[:, j], in0=idx_sum[:, NG:NF, j * PT:(j + 1) * PT], scalar=0.0,
                    in1=vocab_last[:, NG:NF, j * PT:(j + 1) * PT], op0=ALU.max, op1=ALU.min)
            clip(idx_cross[:], NF, NF + NX).then_inc(index_ready, 1)

            for n, (src, rest, parts, ready) in enumerate(splits):
                dve.wait_ge(part_rounded, 2 * n + 1)
                nc.vector.tensor_tensor(rest, src, parts[0], ALU.subtract).then_inc(rest_ready, 1)
                dve.wait_ge(part_rounded, 2 * n + 2)
                nc.vector.tensor_tensor(parts[2], rest, parts[1], ALU.subtract).then_inc(ready, 1)

            dve.wait_ge(consts_ready, 2)

            def build_onehot(j, h, chunks):
                for c in chunks:
                    i = max(k for k in range(NL) if CHUNK0[k] <= c)
                    nc.vector.tensor_scalar(
                        onehot[h][:, c, :], idx_bc[:, bass.ds(j, 1), i, h * BLOCK:(h + 1) * BLOCK],
                        row_id[:, c - CHUNK0[i]:c - CHUNK0[i] + 1], None, ALU.is_equal,
                    ).then_inc(onehot_ready, 1)

            def sum_parts(j, h, s):
                for k, group in enumerate(FGROUPS):
                    dve.wait_ge(looked_up[h], j * BT * NGR + s * NGR + k + 1)
                    nc.vector.tensor_reduce(
                        x[h][:, s, (NG + group[0]) * ROW:(NG + group[-1] + 1) * ROW].rearrange("p (f n) -> p f n", n=ROW),
                        look_ps[k][:].rearrange("p f c n -> p f n c"), AX.X, ALU.add,
                    ).then_inc(looked_up_summed, 1)

            def sum_wide(j, h):
                dve.wait_ge(rows_gathered[h], (j + 1) * (16 * NG * BT))
                dve.wait_ge(looked_up_summed, j * 2 * BT * NGR + (h + 1) * BT * NGR)
                nc.vector.tensor_reduce(wide[:, bass.ds(j * PT + h * BT, BT)],
                                        x[h][:].rearrange("p s (g n) -> p s g n", n=2 * ROW)[:, :, :, 0:2 * ROW:2 * ROW - 1],
                                        AX.XY, ALU.add).then_inc(x_summed[h], 1)

            quarter = -(-NCH // BT)
            dve.wait_ge(index_spread[0], 16)
            with dve.Fori(0, PAIRS) as j:
                build_onehot(j, 0, range(NCH))
                for s in range(BT):
                    sum_parts(j, 0, s)
                    build_onehot(j, 1, range(s * quarter, min((s + 1) * quarter, NCH)))
                for s in range(BT):
                    sum_parts(j, 1, s)
                sum_wide(j, 0)
                sum_wide(j, 1)
                dve.wait_ge(index_spread[PAIRS - 1], 16)
                for h in range(2):
                    dve.wait_ge(turned[h], (j + 1) * KB)

            dve.wait_ge(cross_gathered, 16 * NX * TILES)
            step(nc.vector.tensor_tensor(cross_sum[:], cross[:, 0, :], cross[:, 1, :], ALU.add))
            dve.wait_ge(bias_loaded, 16)
            dve.wait_ge(x_summed[1], PAIRS)
            step(nc.vector.scalar_tensor_tensor(out=wide_sum[:], in0=cross_sum[:], scalar=bias_sb[:, 0:1],
                                                in1=wide[:], op0=ALU.add, op1=ALU.add))
            for h in range(2):
                dve.wait_ge(deep_done[h], PAIRS * BT)
            nc.vector.tensor_tensor(result[:], wide_sum[:], deep_ps[:], ALU.add).then_inc(result_ready, 1)

        @block.tensor
        def _(pe):
            pe.wait_ge(consts_ready, 2)
            pe.wait_ge(index_ready, 1)
            nc.tensor.transpose(tr_ps[0][0:PAIRS * NL * PT, 0:P], idx_look[:].rearrange("p j f t -> p (j f t)"),
                                ident[:]).then_inc(index_turned, 1)
            pe.wait_ge(wd_loaded, 32)
            nc.tensor.matmul(mm_ps[0][0:ND, :], wd_sb[:], w1d_sb[:], start=True, stop=True).then_inc(wdense_done, 1)

            def look_up(j, h, s):
                for k, group in enumerate(FGROUPS):
                    n = (h * BT + s) * NGR + k
                    if s == 0:
                        pe.wait_ge(onehot_ready, j * 2 * NCH + h * NCH + CHUNK_END[k])
                    if n >= NGR:
                        pe.wait_ge(looked_up_summed, j * 2 * BT * NGR + n - NGR + 1)
                    for i in group:
                        for c in range(CHUNKS[i]):
                            last = nc.tensor.matmul(
                                look_ps[k][:, i - group[0], :, :].rearrange("p c n -> p (c n)"),
                                onehot[h][:, CHUNK0[i] + c, s * P:(s + 1) * P],
                                table_parts[:, CHUNK0[i] + c, :, :].rearrange("p c n -> p (c n)"),
                                start=c == 0, stop=c == CHUNKS[i] - 1)
                    last.then_inc(looked_up[h], 1)

            def turn(j, h, g):
                n = h * KB + g
                if g == 0:
                    pe.wait_ge(rows_gathered[h], (j + 1) * (16 * NG * BT))
                if 2 * g + 1 >= NG and (g == 0 or 2 * g - 1 < NG):
                    pe.wait_ge(looked_up_summed, j * 2 * BT * NGR + (h + 1) * BT * NGR)
                if n >= 2:
                    pe.wait_ge(turned_copied, j * 2 * KB + n - 1)
                for s in range(BT):
                    last = nc.tensor.transpose(tr_ps[n % 2][:, s * P:(s + 1) * P],
                                               x[h][:, s, 2 * g * ROW + 1:2 * g * ROW + 1 + 2 * D], ident[:])
                last.then_inc(turned[h], 1)

            def wait_bank(j, turn_):
                if turn_ >= 2:
                    pe.wait_ge(layer_copied, j * TURNS + turn_ - 1)

            def layer1(j, h, m):
                t = L1_TURN[h] + m
                wait_bank(j, t)
                nc.tensor.matmul(mm_ps[t % 2][:], wdense_stack[:, m * P:(m + 1) * P],
                                 dense_stack[:, bass.ds(j * (2 * BLOCK) + h * BLOCK, BLOCK)], start=True, stop=False)
                for g in range(KB):
                    if m == 0:
                        pe.wait_ge(turned_copied, j * 2 * KB + h * KB + g + 1)
                    last = nc.tensor.matmul(mm_ps[t % 2][:], w1_sb[:, g, m * P:(m + 1) * P], xt[h][:, g, :],
                                            start=False, stop=g == KB - 1)
                last.then_inc(layer1_done[h], 1)

            def layer2(j, h):
                for n in range(M2):
                    t = L2_TURN[h] + n
                    wait_bank(j, t)
                    for m in range(M1):
                        if n == 0:
                            pe.wait_ge(layer_copied, j * TURNS + L1_TURN[h] + m + 1)
                        last = nc.tensor.matmul(mm_ps[t % 2][:], w2_sb[:, m, n * P:(n + 1) * P], h1[h][:, m, :],
                                                start=m == 0, stop=m == M1 - 1)
                    last.then_inc(layer2_done[h], 1)

            def layer3(j, h):
                pe.wait_ge(layer_copied, j * TURNS + L2_TURN[h] + M2)
                for s in range(BT):
                    col = h * BT + s
                    acc = deep_ps[:, bass.ds(j * PT + col, 1)]
                    nc.tensor.matmul(acc,
                                     dense_stack[:, bass.ds(j * (2 * BLOCK) + col * P, P)],
                                     wdense_stack[:, H1:H1 + 1], start=True, stop=False)
                    for m in range(M2):
                        last = nc.tensor.matmul(acc, h2[h][:, m, s * P:(s + 1) * P],
                                                w3_sb[:, m:m + 1], start=False, stop=m == M2 - 1)
                    last.then_inc(deep_done[h], 1)

            pe.wait_ge(table_part_ready, 1)
            pe.wait_ge(index_rows_ready, 1)
            with pe.Fori(0, PAIRS) as j:
                for s in range(BT):
                    look_up(j, 0, s)
                for s in range(BT):
                    look_up(j, 1, s)
                    turn(j, 0, s)
                pe.wait_ge(w1_loaded, 16 * NF)
                pe.wait_ge(dense_stacked, 2 * 16 * SPLIT * SPLIT)
                for m in range(M1):
                    layer1(j, 0, m)
                    turn(j, 1, m)
                pe.wait_ge(w23_loaded, 32)
                layer2(j, 0)
                for m in range(M1):
                    layer1(j, 1, m)
                layer3(j, 0)
                layer2(j, 1)
                layer3(j, 1)


def kernel(**inputs):
    import concourse.bacc as bacc
    from concourse.bass_utils import run_bass_kernel_spmd

    a = {k: np.ascontiguousarray(v) for k, v in inputs.items()}
    table = {}
    for k, f in enumerate(FIELDS):
        row = [a[f"L0_rec_w{f}"], a[f"L0_rec_E{f}"]]
        table[f] = np.concatenate(row if k % 2 == 0 else row[::-1], axis=1)
    index = np.stack([a[f"r_s{f}"].reshape(TILES, P) for f in FIELDS])
    small = np.concatenate([np.pad(table[f], ((0, -VOCABS[f] % P), (0, 0))) for f in LOOKED_UP])
    w1 = a["L0_rec_W1"]
    arrays = {
        "index": index.transpose(2, 0, 1),
        "dense_t": a["r_dense"].T,
        "small": small.reshape(NCH, P, ROW).transpose(1, 0, 2),
        "wd_deep_t": a["L0_rec_Wd_deep"].T,
        "wd_wide": a["L0_rec_Wd_wide"],
        "w1": w1,
        "w2": a["L0_rec_W2"],
        "w3": a["L0_rec_W3"].reshape(M2, P).T,
        "bias": a["L0_rec_bias"],
    }
    for f in GATHERED:
        arrays[f"rows{f}"] = table[f]
    for c in range(NX):
        arrays[f"wc{c}"] = a[f"L0_rec_wc{c}"]
    arrays = {f"in_{k}_dram": np.ascontiguousarray(v) for k, v in arrays.items()}

    nc = bacc.Bacc("TRN2", target_bir_lowering=False, num_devices=1)
    ap = {k: nc.dram_tensor(k, v.shape, mybir.dt.from_np(v.dtype), kind="ExternalInput").ap()
          for k, v in arrays.items()}
    out = nc.dram_tensor("out_dram", (P, TILES), mybir.dt.float32, kind="ExternalOutput").ap()

    def one(name):
        return ap[f"in_{name}_dram"]

    program(nc, one("index"), one("dense_t"), [one(f"rows{f}") for f in GATHERED], one("small"),
            [one(f"wc{c}") for c in range(NX)], one("wd_deep_t"), one("wd_wide"), one("w1"), one("w2"),
            one("w3"), one("bias"), out)
    r = run_bass_kernel_spmd(nc, [arrays], core_ids=[0])
    return np.ascontiguousarray(r.results[0]["out_dram"].T).reshape(BATCH, 1)
```

```python
import numpy as np

import concourse.bass as bass
from concourse import mybir
from contextlib import ExitStack

P = 128
BATCH = 2048
D = 64
ND = 13
VOCABS = [125000, 25000, 12500, 375, 375, 1000, 500, 100]
H1, H2 = 512, 256

GATHERED = [0, 1, 2]
LOOKED_UP = [3, 4, 5, 6, 7]
FIELDS = GATHERED + LOOKED_UP
NG, NL, NF = len(GATHERED), len(LOOKED_UP), len(FIELDS)
ROW = D + 1
CROSSES = [(3, 4), (5, 6)]
NX = len(CROSSES)
SPLIT = 3

TILES = BATCH // P
BLOCK = 512
BT = BLOCK // P
BLOCKS = BATCH // BLOCK
PAIR = 2 * BLOCK
PT = 2 * BT

CHUNKS = [-(-VOCABS[f] // P) for f in LOOKED_UP]
CHUNK0 = [sum(CHUNKS[:i]) for i in range(NL)]
NCH = sum(CHUNKS)
GROUPS = [list(range(i, min(i + 2, NL))) for i in range(0, NL, 2)]
NGR = len(GROUPS)
UNITS = NGR * PT
CHUNK_END = [CHUNK0[g[-1]] + CHUNKS[g[-1]] for g in GROUPS]
LOOK_BANKS = 3
SPREADS = NL * 2
KB = NF * D // P
M1, M2 = H1 // P, H2 // P
TURNS = M1 + M2
NROWS = SPLIT * SPLIT * ND
DFOLD = 8

SPREAD_SLOTS = [range(0, 3), range(3, 6), range(6, 8), range(8, 10)]
ONEHOT_SLOTS = [range(0, 0), range(0, 3), range(3, 9), range(9, 14)]
ONEHOT_REST = range(14, NCH)
LOOK_SLOTS = [range(0, 8), range(8, 24)]


def program(nc, index, dense_t, big, small, wc, wd_deep_t, wd_wide, w1, w2, w3, bias, out):
    f32, bf16, f16, i32 = mybir.dt.float32, mybir.dt.bfloat16, mybir.dt.float16, mybir.dt.int32
    f32r = mybir.dt.float32r
    ALU, ACT, AX = mybir.AluOpType, mybir.ActivationFunctionType, mybir.AxisListType
    dense_dram = nc.dram_tensor("dense_dram", (SPLIT, ND, BATCH), bf16, kind="Internal").ap()

    with ExitStack() as ctx:
        def sb(name, shape, dt):
            return ctx.enter_context(nc.sbuf_tensor(name, shape, dt))

        def pb(name, shape):
            return ctx.enter_context(nc.psum_tensor(name, shape, f32))

        def sem(name):
            return ctx.enter_context(nc.semaphore(name))

        idx_raw = sb("idx_raw", [P, NF, TILES], i32)
        idx_f = sb("idx_f", [P, NF + NX, TILES], f32)
        idx_wrap = sb("idx_wrap", [P, NF + NX, TILES], f32)
        idx_sum = sb("idx_sum", [P, NF + NX, TILES], f32)
        vocab = sb("vocab", [P, NF + NX, TILES], f32)
        vocab_last = sb("vocab_last", [P, NF + NX, TILES], f32)
        idx_gather = sb("idx_gather", [P, NG, TILES], i32)
        idx_cross = sb("idx_cross", [P, NX, TILES], i32)
        idx_look = sb("idx_look", [P, NL, TILES], f16)
        idx_bc = sb("idx_bc", [P, NL, PAIR], f16)
        zero = sb("zero", [P, P], f32)
        ident = sb("ident", [P, P], f32)
        ident16 = sb("ident16", [P, P], f16)
        row_id = sb("row_id", [P, max(CHUNKS)], f32)
        table = sb("table", [P, NCH, ROW], f32)
        table_parts = sb("table_parts", [P, NCH, SPLIT, ROW], bf16)
        onehot = sb("onehot", [P, NCH, PAIR], bf16)
        dense_sb = sb("dense_sb", [ND * DFOLD, BATCH // DFOLD], f32)
        dense_parts = sb("dense_parts", [ND * DFOLD, SPLIT, BATCH // DFOLD], bf16)
        dense_stack = sb("dense_stack", [NROWS, BATCH], bf16)
        wd_sb = sb("wd_sb", [D, ND], f32)
        w1d_sb = sb("w1d_sb", [D, H1], f32)
        wdense = sb("wdense", [ND, H1 + 1], f32)
        wdense_parts = sb("wdense_parts", [ND, SPLIT, H1 + 1], bf16)
        wdense_stack = sb("wdense_stack", [NROWS, H1 + 1], bf16)
        w1_sb = sb("w1_sb", [P, KB, H1], f32)
        w1_hi = sb("w1_hi", [P, KB, H1], f32r)
        w1_lo = sb("w1_lo", [P, KB, H1], f32r)
        w2_sb = sb("w2_sb", [P, M1, H2], f32)
        w2_hi = sb("w2_hi", [P, M1, H2], f32r)
        w2_lo = sb("w2_lo", [P, M1, H2], f32r)
        w3_sb = sb("w3_sb", [P, M2], f32)
        bias_sb = sb("bias_sb", [P, 1], f32)
        x = sb("x", [P, TILES, NF * ROW], f32)
        xt_hi = [sb(f"xt_hi{h}", [P, KB, BLOCK], f32r) for h in range(2)]
        xt_lo = [sb(f"xt_lo{h}", [P, KB, BLOCK], f32r) for h in range(2)]
        h1_hi = sb("h1_hi", [P, M1, BLOCK], f32r)
        h1_lo = sb("h1_lo", [P, M1, BLOCK], f32r)
        h2 = sb("h2", [P, M2, BLOCK], f32)
        wide = sb("wide", [P, TILES], f32)
        cross = sb("cross", [P, NX, TILES], f32)
        cross_sum = sb("cross_sum", [P, TILES], f32)
        wide_sum = sb("wide_sum", [P, TILES], f32)
        result = sb("result", [P, TILES], f32)

        look_ps = [pb(f"look_ps{k}", [P, BLOCK]) for k in range(LOOK_BANKS)]
        tr_ps = [pb(f"tr_ps{k}", [P, BLOCK]) for k in range(2)]
        mm_ps = [pb(f"mm_ps{k}", [P, BLOCK]) for k in range(2)]
        deep_ps = pb("deep_ps", [P, TILES])

        index_loaded = sem("index_loaded")
        table_loaded = [sem(f"table_loaded{k}") for k in range(2)]
        dense_loaded = sem("dense_loaded")
        wd_loaded = sem("wd_loaded")
        wide_weight_loaded = sem("wide_weight_loaded")
        w1_loaded = sem("w1_loaded")
        w2_loaded = sem("w2_loaded")
        w3_loaded = sem("w3_loaded")
        bias_loaded = sem("bias_loaded")
        zero_ready = sem("zero_ready")
        ident_ready = sem("ident_ready")
        row_id_ready = sem("row_id_ready")
        vocab_ready = sem("vocab_ready")
        index_ready = sem("index_ready")
        index_spread = sem("index_spread")
        index_copied = sem("index_copied")
        wdense_done = sem("wdense_done")
        wdense_copied = sem("wdense_copied")
        part_rounded = sem("part_rounded")
        rest_ready = sem("rest_ready")
        part_last = sem("part_last")
        table_first_ready = sem("table_first_ready")
        dense_stored = sem("dense_stored")
        dense_stacked = sem("dense_stacked")
        w1_high = sem("w1_high")
        w1_low = sem("w1_low")
        w2_high = sem("w2_high")
        w2_low = sem("w2_low")
        rows_gathered = [sem(f"rows_gathered{b}") for b in range(BLOCKS)]
        cross_gathered = sem("cross_gathered")
        onehot_ready = sem("onehot_ready")
        looked_up = sem("looked_up")
        rows_copied = sem("rows_copied")
        rows_summed = sem("rows_summed")
        turned = sem("turned")
        turned_high = sem("turned_high")
        turned_low = sem("turned_low")
        layer_done = sem("layer_done")
        layer1_low = sem("layer1_low")
        layer_high = sem("layer_high")
        deep_done = sem("deep_done")
        wide_ready = sem("wide_ready")
        vector_step = sem("vector_step")
        result_ready = sem("result_ready")
        result_stored = sem("result_stored")

        CA = CHUNK_END[0]
        splits = [
            (table[:, CA:], [table_parts[:, CA:, i, :] for i in range(SPLIT)]),
            (dense_sb[:], [dense_parts[:, i, :] for i in range(SPLIT)]),
            (wdense[:], [wdense_parts[:, i, :] for i in range(SPLIT)]),
        ]
        TABLE, DENSE, WDENSE = range(3)

        def unit(n):
            return n // PT, n % PT

        def merged(pair, n):
            return pair == 0 and unit(n)[0] != 1

        def written(pair, n):
            kind = merged(pair, n)
            count = sum(merged(p, i) == kind for p in range(pair + 1) for i in range(UNITS if p < pair else n + 1))
            return (rows_copied if kind else rows_summed), count

        block = ctx.enter_context(nc.Block())

        @block.sync
        def _(sp):
            sp.dma_start(idx_raw[:], index).then_inc(index_loaded, 16)
            sp.dma_start(table[:, 0:CA], small[:, 0:CA]).then_inc(table_loaded[0], 16)
            sp.dma_start(table[:, CA:], small[:, CA:]).then_inc(table_loaded[1], 16)
            sp.dma_start(wd_sb[:], wd_deep_t).then_inc(wd_loaded, 16)
            sp.dma_start(w1d_sb[:], w1[0:D, :]).then_inc(wd_loaded, 16)
            sp.dma_start(dense_sb[:], dense_t.rearrange("k (b n) -> (k b) n", b=DFOLD)).then_inc(dense_loaded, 16)
            sp.dma_start(wdense[:, H1:H1 + 1], wd_wide).then_inc(wide_weight_loaded, 16)
            sp.dma_start(w1_sb[:], w1[D:, :].rearrange("(k p) n -> p k n", p=P)).then_inc(w1_loaded, 16)
            sp.dma_start(w2_sb[:], w2.rearrange("(k p) n -> p k n", p=P)).then_inc(w2_loaded, 16)
            sp.dma_start(w3_sb[:], w3).then_inc(w3_loaded, 16)
            sp.dma_start(bias_sb[:], bias.to_broadcast([P, 1])).then_inc(bias_loaded, 16)
            sp.wait_ge(part_last, DENSE + 1)
            sp.dma_start(dense_dram.rearrange("s k (b n) -> (k b) s n", b=DFOLD), dense_parts[:])\
              .then_inc(dense_stored, 16)
            sp.wait_ge(dense_stored, 16)
            for a in range(SPLIT):
                for b in range(SPLIT):
                    r = (a * SPLIT + b) * ND
                    sp.dma_start(dense_stack[r:r + ND, :], dense_dram[a]).then_inc(dense_stacked, 16)
            sp.wait_ge(part_last, WDENSE + 1)
            for a in range(SPLIT):
                for b in range(SPLIT):
                    r = (a * SPLIT + b) * ND
                    sp.dma_start(wdense_stack[r:r + ND, :], wdense_parts[:, b, :]).then_inc(dense_stacked, 16)
            sp.wait_ge(result_ready, 1)
            sp.dma_start(out, result[:]).then_inc(result_stored, 16)
            sp.wait_ge(result_stored, 16)

        @block.gpsimd
        def _(pool):
            nc.gpsimd.memset(zero[:], 0.0).then_inc(zero_ready, 1)
            nc.gpsimd.iota(row_id[:], pattern=[[P, max(CHUNKS)]], base=0, channel_multiplier=1,
                           allow_small_or_imprecise_dtypes=True).then_inc(row_id_ready, 1)
            pool.wait_ge(zero_ready, 1)
            for m in (ident16, ident):
                nc.gpsimd.affine_select(out=m[:], in_=zero[:], compare_op=ALU.not_equal, fill=1.0, base=0,
                                        pattern=[[-1, P]], channel_multiplier=1).then_inc(ident_ready, 1)
            pool.wait_ge(index_ready, 2)
            for t in range(TILES):
                for g in range(NG):
                    nc.gpsimd.indirect_dma_start(
                        out=x[:, t, g * ROW:(g + 1) * ROW], out_offset=None, in_=big[g],
                        in_offset=bass.IndirectOffsetOnAxis(ap=idx_gather[:, g, t:t + 1], axis=0),
                    ).then_inc(rows_gathered[t // BT], 16)
            pool.wait_ge(index_ready, 3)
            for c in range(NX):
                for t in range(TILES):
                    nc.gpsimd.indirect_dma_start(
                        out=cross[:, c, t:t + 1], out_offset=None, in_=wc[c],
                        in_offset=bass.IndirectOffsetOnAxis(ap=idx_cross[:, c, t:t + 1], axis=0),
                    ).then_inc(cross_gathered, 16)

        @block.scalar
        def _(act):
            def copy_spread(pair, n):
                i, h = n // 2, n % 2
                act.wait_ge(index_spread, pair * SPREADS + n + 1)
                if pair and h == 0:
                    act.wait_ge(onehot_ready, CHUNK0[i] + CHUNKS[i])
                nc.scalar.copy(idx_bc[:, i, h * BLOCK:(h + 1) * BLOCK], look_ps[n % LOOK_BANKS][:])\
                    .then_inc(index_copied, 1)

            def first_part(n):
                src, parts = splits[n]
                nc.scalar.copy(parts[0], src).then_inc(part_rounded, 1)

            def second_part(n):
                src, parts = splits[n]
                act.wait_ge(rest_ready, n + 1)
                nc.scalar.copy(parts[1], src).then_inc(part_rounded, 1)

            def turned_hi(b, g):
                n = b * KB + g
                act.wait_ge(turned, n + 1)
                nc.scalar.copy(xt_hi[b % 2][:, g, :], tr_ps[n % 2][:]).then_inc(turned_high, 1)

            def relu(n, dst):
                act.wait_ge(layer_done, n + 1)
                nc.scalar.activation(dst, mm_ps[n % 2][:], ACT.Relu).then_inc(layer_high, 1)

            def copy_rows(n):
                k, t = unit(n)
                lo, hi = (NG + GROUPS[k][0]) * ROW, (NG + GROUPS[k][-1] + 1) * ROW
                act.wait_ge(looked_up, n + 1)
                nc.scalar.copy(x[:, t, lo:hi], look_ps[n % LOOK_BANKS][:, 0:hi - lo]).then_inc(rows_copied, 1)

            for n in range(SPREADS):
                copy_spread(0, n)
                if n == 3:
                    act.wait_ge(table_loaded[1], 16)
                    first_part(TABLE)
            second_part(TABLE)
            act.wait_ge(wdense_done, 1)
            nc.scalar.copy(wdense[:, 0:H1], mm_ps[0][0:ND, :]).then_inc(wdense_copied, 1)
            for n in range(PT):
                copy_rows(n)
            act.wait_ge(dense_loaded, 16)
            first_part(DENSE)
            second_part(DENSE)
            act.wait_ge(wdense_copied, 1)
            act.wait_ge(wide_weight_loaded, 16)
            first_part(WDENSE)
            second_part(WDENSE)
            act.wait_ge(w1_loaded, 16)
            for g in range(KB):
                nc.scalar.copy(w1_hi[:, g, :], w1_sb[:, g, :]).then_inc(w1_high, 1)
            act.wait_ge(w2_loaded, 16)
            nc.scalar.copy(w2_hi[:], w2_sb[:]).then_inc(w2_high, 1)
            turned_hi(0, 0)
            for n in range(2 * PT, UNITS):
                copy_rows(n)
            for g in range(1, KB):
                turned_hi(0, g)
            for b in range(BLOCKS):
                for m in range(M1):
                    relu(b * TURNS + m, h1_hi[:, m, :])
                    if b + 1 < BLOCKS:
                        turned_hi(b + 1, m)
                    if b == 0:
                        for n in SPREAD_SLOTS[m]:
                            copy_spread(1, n)
                for m in range(M2):
                    relu(b * TURNS + M1 + m, h2[:, m, :])

        @block.vector
        def _(dve):
            steps = [0]

            def step(ins):
                steps[0] += 1
                ins.then_inc(vector_step, 1)
                dve.wait_ge(vector_step, steps[0])

            sizes = [VOCABS[f] for f in FIELDS] + [VOCABS[a] * VOCABS[b] for a, b in CROSSES]
            for k, v in enumerate(sizes):
                nc.vector.memset(vocab[:, k, :], float(v)).then_inc(vocab_ready, 1)
                nc.vector.memset(vocab_last[:, k, :], float(v - 1)).then_inc(vocab_ready, 1)
            dve.wait_ge(index_loaded, 16)
            step(nc.vector.tensor_copy(idx_f[:, 0:NF, :], idx_raw[:]))
            for c, (a, b) in enumerate(CROSSES):
                ins = nc.vector.scalar_tensor_tensor(
                    out=idx_f[:, NF + c, :], in0=idx_f[:, FIELDS.index(a), :], scalar=float(VOCABS[b]),
                    in1=idx_f[:, FIELDS.index(b), :], op0=ALU.mult, op1=ALU.add)
            step(ins)
            dve.wait_ge(vocab_ready, 2 * len(sizes))
            step(nc.vector.scalar_tensor_tensor(out=idx_wrap[:], in0=idx_f[:], scalar=0.0, in1=vocab[:],
                                                op0=ALU.is_lt, op1=ALU.mult))
            step(nc.vector.tensor_tensor(idx_sum[:], idx_wrap[:], idx_f[:], ALU.add))
            for dst, lo, hi in ((idx_look, NG, NF), (idx_gather, 0, NG), (idx_cross, NF, NF + NX)):
                nc.vector.scalar_tensor_tensor(out=dst[:], in0=idx_sum[:, lo:hi], scalar=0.0,
                                               in1=vocab_last[:, lo:hi], op0=ALU.max, op1=ALU.min)\
                    .then_inc(index_ready, 1)

            def build_onehot(pair, chunks):
                for c in chunks:
                    i = max(k for k in range(NL) if CHUNK0[k] <= c)
                    if c == CHUNK0[i]:
                        dve.wait_ge(index_copied, pair * SPREADS + 2 * i + 2)
                    nc.vector.tensor_scalar(
                        onehot[:, c, :], idx_bc[:, i, :], row_id[:, c - CHUNK0[i]:c - CHUNK0[i] + 1],
                        None, ALU.is_equal).then_inc(onehot_ready, 1)

            def first_rest(n):
                src, parts = splits[n]
                dve.wait_ge(part_rounded, 2 * n + 1)
                nc.vector.tensor_tensor(src, src, parts[0], ALU.subtract).then_inc(rest_ready, 1)

            def last_part(n):
                src, parts = splits[n]
                dve.wait_ge(part_rounded, 2 * n + 2)
                dve.wait_ge(rest_ready, n + 1)
                nc.vector.tensor_tensor(parts[2], src, parts[1], ALU.subtract).then_inc(part_last, 1)

            def weight_low(dst, src, hi, ready, count, done):
                dve.wait_ge(ready, count)
                nc.vector.tensor_tensor(dst, src, hi.bitcast(f32), ALU.subtract).then_inc(done, 1)

            def sum_parts(pair, n):
                k, t = unit(n)
                group = GROUPS[k]
                dve.wait_ge(looked_up, pair * UNITS + n + 1)
                nc.vector.tensor_reduce(
                    x[:, pair * PT + t, (NG + group[0]) * ROW:(NG + group[-1] + 1) * ROW]
                    .rearrange("p (f n) -> p f n", n=ROW),
                    look_ps[n % LOOK_BANKS][:, 0:len(group) * SPLIT * ROW]
                    .rearrange("p (f c n) -> p f n c", c=SPLIT, n=ROW), AX.X, ALU.add,
                ).then_inc(rows_summed, 1)

            def turned_lo(b, g):
                n = b * KB + g
                dve.wait_ge(turned_high, n + 1)
                nc.vector.tensor_tensor(xt_lo[b % 2][:, g, :], tr_ps[n % 2][:], xt_hi[b % 2][:, g, :].bitcast(f32),
                                        ALU.subtract).then_inc(turned_low, 1)

            def relu_lo(b, m):
                n = b * TURNS + m
                dve.wait_ge(layer_high, n + 1)
                nc.vector.scalar_tensor_tensor(out=h1_lo[:, m, :], in0=mm_ps[n % 2][:], scalar=0.0,
                                               in1=h1_hi[:, m, :].bitcast(f32), op0=ALU.max,
                                               op1=ALU.subtract).then_inc(layer1_low, 1)

            first = table[:, 0:CA]
            parts = [table_parts[:, 0:CA, i, :] for i in range(SPLIT)]
            dve.wait_ge(table_loaded[0], 16)
            step(nc.vector.tensor_copy(parts[0], first))
            step(nc.vector.tensor_tensor(first, first, parts[0], ALU.subtract))
            step(nc.vector.tensor_copy(parts[1], first))
            nc.vector.tensor_tensor(parts[2], first, parts[1], ALU.subtract).then_inc(table_first_ready, 1)

            dve.wait_ge(row_id_ready, 1)
            build_onehot(0, range(0, CA))
            first_rest(TABLE)
            build_onehot(0, range(CA, CHUNK0[3]))
            last_part(TABLE)
            build_onehot(0, range(CHUNK0[3], NCH))
            for n in range(PT, 2 * PT):
                sum_parts(0, n)
                t = unit(n)[1]
                if t == 0:
                    first_rest(DENSE)
                if t == 1:
                    last_part(DENSE)
                if t == 2:
                    first_rest(WDENSE)
                if t == 3:
                    last_part(WDENSE)
                if t >= PT - KB:
                    g = t - (PT - KB)
                    weight_low(w1_lo[:, g, :], w1_sb[:, g, :], w1_hi[:, g, :], w1_high, g + 1, w1_low)
            for g in range(KB):
                turned_lo(0, g)
            weight_low(w2_lo[:], w2_sb[:], w2_hi[:], w2_high, 1, w2_low)
            for b in range(BLOCKS):
                for m in range(M1):
                    relu_lo(b, m)
                    if b + 1 < BLOCKS:
                        turned_lo(b + 1, m)
                    if b == 0:
                        build_onehot(1, ONEHOT_SLOTS[m])
                if b == 0:
                    build_onehot(1, ONEHOT_REST)
                    for m in range(M2):
                        for n in LOOK_SLOTS[m]:
                            sum_parts(1, n)

            for b in range(BLOCKS):
                dve.wait_ge(rows_gathered[b], 16 * NG * BT)
            for kind in range(2):
                dve.wait_ge(*written(kind, UNITS - 1))
            nc.vector.tensor_reduce(
                wide[:], x[:].rearrange("p t (g n) -> p t g n", n=2 * ROW)[:, :, :, 0:2 * ROW:2 * ROW - 1],
                AX.XY, ALU.add).then_inc(wide_ready, 1)
            dve.wait_ge(cross_gathered, 16 * NX * TILES)
            step(nc.vector.tensor_tensor(cross_sum[:], cross[:, 0, :], cross[:, 1, :], ALU.add))
            dve.wait_ge(bias_loaded, 16)
            dve.wait_ge(wide_ready, 1)
            step(nc.vector.scalar_tensor_tensor(out=wide_sum[:], in0=cross_sum[:], scalar=bias_sb[:, 0:1],
                                                in1=wide[:], op0=ALU.add, op1=ALU.add))
            dve.wait_ge(deep_done, BLOCKS)
            nc.vector.tensor_tensor(result[:], wide_sum[:], deep_ps[:], ALU.add).then_inc(result_ready, 1)

        @block.tensor
        def _(pe):
            def spread_index(pair, n):
                i, h = n // 2, n % 2
                if n >= LOOK_BANKS:
                    pe.wait_ge(index_copied, pair * SPREADS + n - LOOK_BANKS + 1)
                elif pair:
                    pe.wait_ge(*written(0, UNITS - LOOK_BANKS + n))
                for s in range(BT):
                    t = pair * PT + h * BT + s
                    last = nc.tensor.matmul(look_ps[n % LOOK_BANKS][:, s * P:(s + 1) * P],
                                            idx_look[:, i, t:t + 1].to_broadcast([P, P]), ident16[:],
                                            start=True, stop=True)
                last.then_inc(index_spread, 1)

            def look_up(pair, n):
                k, t = unit(n)
                if t == 0:
                    pe.wait_ge(onehot_ready, pair * NCH + CHUNK_END[k])
                if n >= LOOK_BANKS:
                    pe.wait_ge(*written(pair, n - LOOK_BANKS))
                elif n == 0:
                    pe.wait_ge(index_copied, (pair + 1) * SPREADS)
                group = GROUPS[k]
                for i in group:
                    rows = table_parts[:, CHUNK0[i]:CHUNK0[i] + CHUNKS[i], :, :]
                    if merged(pair, n):
                        at = (i - group[0]) * ROW
                        passes = [(c, rows[:, c, p, :]) for c in range(CHUNKS[i]) for p in range(SPLIT)]
                    else:
                        at = (i - group[0]) * SPLIT * ROW
                        passes = [(c, rows[:, c, :, :].rearrange("p c n -> p (c n)")) for c in range(CHUNKS[i])]
                    for q, (c, part) in enumerate(passes):
                        last = nc.tensor.matmul(look_ps[n % LOOK_BANKS][:, at:at + part.shape[-1]],
                                                onehot[:, CHUNK0[i] + c, t * P:(t + 1) * P], part,
                                                start=q == 0, stop=q == len(passes) - 1)
                last.then_inc(looked_up, 1)

            def turn(b, g):
                n = b * KB + g
                if g == 0:
                    pe.wait_ge(rows_gathered[b], 16 * NG * BT)
                for k, group in enumerate(GROUPS):
                    if any(NG + i in (2 * g, 2 * g + 1) for i in group):
                        pe.wait_ge(*written(b // 2, (k + 1) * PT - 1))
                if n >= 2:
                    pe.wait_ge(turned_low, n - 1)
                for s in range(BT):
                    last = nc.tensor.transpose(tr_ps[n % 2][:, s * P:(s + 1) * P],
                                               x[:, b * BT + s, 2 * g * ROW + 1:2 * g * ROW + 1 + 2 * D], ident[:])
                last.then_inc(turned, 1)

            def wait_bank(n):
                if n >= 2:
                    pe.wait_ge(layer_high, n - 1)
                    b, m = (n - 2) // TURNS, (n - 2) % TURNS
                    if m < M1:
                        pe.wait_ge(layer1_low, b * M1 + m + 1)

            def product(dst, w_hi, w_lo, a_hi, a_lo, start, stop):
                nc.tensor.matmul(dst, w_hi, a_hi, start=start, stop=False)
                nc.tensor.matmul(dst, w_hi, a_lo, start=False, stop=False)
                return nc.tensor.matmul(dst, w_lo, a_hi, start=False, stop=stop)

            def layer1(b, m):
                n = b * TURNS + m
                wait_bank(n)
                nc.tensor.matmul(mm_ps[n % 2][:], wdense_stack[:, m * P:(m + 1) * P],
                                 dense_stack[:, b * BLOCK:(b + 1) * BLOCK], start=True, stop=False)
                c = slice(m * P, (m + 1) * P)
                for g in range(KB):
                    if b == 0 and m == 0:
                        pe.wait_ge(w1_low, g + 1)
                    if m == 0:
                        pe.wait_ge(turned_low, b * KB + g + 1)
                    last = product(mm_ps[n % 2][:], w1_hi[:, g, c], w1_lo[:, g, c], xt_hi[b % 2][:, g, :],
                                   xt_lo[b % 2][:, g, :], False, g == KB - 1)
                last.then_inc(layer_done, 1)

            def layer2(b, m):
                n = b * TURNS + M1 + m
                wait_bank(n)
                c = slice(m * P, (m + 1) * P)
                for k in range(M1):
                    if m == 0:
                        pe.wait_ge(layer1_low, b * M1 + k + 1)
                    last = product(mm_ps[n % 2][:], w2_hi[:, k, c], w2_lo[:, k, c], h1_hi[:, k, :],
                                   h1_lo[:, k, :], k == 0, k == M1 - 1)
                last.then_inc(layer_done, 1)

            def layer3(b):
                pe.wait_ge(layer_high, (b + 1) * TURNS)
                for s in range(BT):
                    t = b * BT + s
                    nc.tensor.matmul(deep_ps[:, t:t + 1], dense_stack[:, t * P:(t + 1) * P],
                                     wdense_stack[:, H1:H1 + 1], start=True, stop=False)
                    for m in range(M2):
                        last = nc.tensor.matmul(deep_ps[:, t:t + 1], h2[:, m, s * P:(s + 1) * P],
                                                w3_sb[:, m:m + 1], start=False, stop=m == M2 - 1)
                last.then_inc(deep_done, 1)

            pe.wait_ge(ident_ready, 2)
            pe.wait_ge(index_ready, 1)
            for n in range(SPREADS):
                spread_index(0, n)
            pe.wait_ge(wd_loaded, 32)
            nc.tensor.matmul(mm_ps[0][0:ND, :], wd_sb[:], w1d_sb[:], start=True, stop=True).then_inc(wdense_done, 1)
            pe.wait_ge(table_first_ready, 1)
            for n in range(UNITS):
                if n == PT:
                    pe.wait_ge(part_last, TABLE + 1)
                if n == 2 * PT:
                    turn(0, 0)
                look_up(0, n)
            for g in range(1, KB):
                turn(0, g)
            pe.wait_ge(wdense_copied, 1)
            pe.wait_ge(dense_stacked, 2 * 16 * SPLIT * SPLIT)
            for b in range(BLOCKS):
                for m in range(M1):
                    layer1(b, m)
                    if m == 0 and b > 0:
                        layer3(b - 1)
                    if b + 1 < BLOCKS:
                        turn(b + 1, m)
                    if b == 0:
                        for n in SPREAD_SLOTS[m]:
                            spread_index(1, n)
                if b == 0:
                    pe.wait_ge(w2_low, 1)
                    pe.wait_ge(w3_loaded, 16)
                for m in range(M2):
                    layer2(b, m)
                    if b == 0:
                        for n in LOOK_SLOTS[m]:
                            look_up(1, n)
            layer3(BLOCKS - 1)


def kernel(**inputs):
    import concourse.bacc as bacc
    from concourse.bass_utils import run_bass_kernel_spmd

    a = {k: np.ascontiguousarray(v) for k, v in inputs.items()}
    table = {}
    for k, f in enumerate(FIELDS):
        row = [a[f"L0_rec_w{f}"], a[f"L0_rec_E{f}"]]
        table[f] = np.concatenate(row if k % 2 == 0 else row[::-1], axis=1)
    index = np.stack([a[f"r_s{f}"].reshape(TILES, P) for f in FIELDS])
    small = np.concatenate([np.pad(table[f], ((0, -VOCABS[f] % P), (0, 0))) for f in LOOKED_UP])
    w1 = a["L0_rec_W1"]
    arrays = {
        "index": index.transpose(2, 0, 1),
        "dense_t": a["r_dense"].T,
        "small": small.reshape(NCH, P, ROW).transpose(1, 0, 2),
        "wd_deep_t": a["L0_rec_Wd_deep"].T,
        "wd_wide": a["L0_rec_Wd_wide"],
        "w1": w1,
        "w2": a["L0_rec_W2"],
        "w3": a["L0_rec_W3"].reshape(M2, P).T,
        "bias": a["L0_rec_bias"],
    }
    for f in GATHERED:
        arrays[f"rows{f}"] = table[f]
    for c in range(NX):
        arrays[f"wc{c}"] = a[f"L0_rec_wc{c}"]
    arrays = {f"in_{k}_dram": np.ascontiguousarray(v) for k, v in arrays.items()}

    nc = bacc.Bacc("TRN2", target_bir_lowering=False, num_devices=1)
    ap = {k: nc.dram_tensor(k, v.shape, mybir.dt.from_np(v.dtype), kind="ExternalInput").ap()
          for k, v in arrays.items()}
    out = nc.dram_tensor("out_dram", (P, TILES), mybir.dt.float32, kind="ExternalOutput").ap()

    def one(name):
        return ap[f"in_{name}_dram"]

    program(nc, one("index"), one("dense_t"), [one(f"rows{f}") for f in GATHERED], one("small"),
            [one(f"wc{c}") for c in range(NX)], one("wd_deep_t"), one("wd_wide"), one("w1"), one("w2"),
            one("w3"), one("bias"), out)
    r = run_bass_kernel_spmd(nc, [arrays], core_ids=[0])
    return np.ascontiguousarray(r.results[0]["out_dram"].T).reshape(BATCH, 1)
```

```python
import numpy as np

import concourse.bass as bass
from concourse import mybir
from contextlib import ExitStack

P = 128
BATCH = 2048
D = 64
ND = 13
VOCABS = [125000, 25000, 12500, 375, 375, 1000, 500, 100]
H1, H2 = 512, 256

GATHERED = [0, 1, 2, 5]
LOOKED_UP = [3, 4, 6, 7]
FIELDS = GATHERED + LOOKED_UP
NG, NL, NF = len(GATHERED), len(LOOKED_UP), len(FIELDS)
ROW = D + 1
CROSSES = [(3, 4), (5, 6)]
NX = len(CROSSES)
SPLIT = 3

TILES = BATCH // P
BLOCK = 512
BT = BLOCK // P
BLOCKS = BATCH // BLOCK
PAIR = 2 * BLOCK
PT = 2 * BT

CHUNKS = [-(-VOCABS[f] // P) for f in LOOKED_UP]
CHUNK0 = [sum(CHUNKS[:i]) for i in range(NL)]
NCH = sum(CHUNKS)
GROUPS = [[0, 1], [2, 3]]
NGR = len(GROUPS)
UNITS = NGR * PT
BUILT = [c + n for c, n in zip(CHUNK0, CHUNKS)]
LOOK_BANKS = 3
SPREADS = NL * 2
KB = NF * D // P
TURN_ORDER = [2, 0, 3, 1]
M1, M2 = H1 // P, H2 // P
TURNS = M1 + M2
NROWS = SPLIT * SPLIT * ND
DFOLD = 8

MERGED = 10
WDENSE_AFTER = [10, 12]
FIRST_TURN_AFTER = 12
WARM_UP = 6
SPREAD_SLOTS = [range(5, 7), range(7, 8)]
ONEHOT_FIRST = range(0, 3)
ONEHOT_SLOTS = [range(0, 0), range(3, 6), range(6, 9), range(9, 11)]
LOOK_SLOTS = [range(0, 0)] * 2 + [range(0, 2), range(2, 4), range(4, 7), range(7, 10), range(10, 12), range(12, 14),
                                  range(14, 16)]


def slot(slots, n):
    return slots[n] if n < len(slots) else range(0)


def program(nc, index, dense_t, big, small, wc, wd_deep_t, wd_wide, w1, w2, w3, bias, out):
    f32, bf16, f16, i32 = mybir.dt.float32, mybir.dt.bfloat16, mybir.dt.float16, mybir.dt.int32
    f32r = mybir.dt.float32r
    ALU, ACT, AX = mybir.AluOpType, mybir.ActivationFunctionType, mybir.AxisListType
    dense_dram = nc.dram_tensor("dense_dram", (SPLIT, ND, BATCH), bf16, kind="Internal").ap()

    with ExitStack() as ctx:
        def sb(name, shape, dt):
            return ctx.enter_context(nc.sbuf_tensor(name, shape, dt))

        def pb(name, shape):
            return ctx.enter_context(nc.psum_tensor(name, shape, f32))

        def sem(name):
            return ctx.enter_context(nc.semaphore(name))

        idx_raw = sb("idx_raw", [P, NF, TILES], i32)
        idx_pair = sb("idx_pair", [P, NX, TILES], f32)
        idx_wrap = sb("idx_wrap", [P, NF + NX, TILES], f32)
        idx_sum = sb("idx_sum", [P, NF + NX, TILES], f32)
        vocab = sb("vocab", [P, NF + NX, TILES], f32)
        vocab_last = sb("vocab_last", [P, NF + NX, TILES], f32)
        idx_gather = sb("idx_gather", [P, NG, TILES], i32)
        idx_cross = sb("idx_cross", [P, NX, TILES], i32)
        idx_look = sb("idx_look", [P, NL, TILES], f16)
        idx_bc = sb("idx_bc", [P, NL, PAIR], f16)
        zero = sb("zero", [P, P], f32)
        zero16 = sb("zero16", [P, BLOCK], bf16)
        ident = sb("ident", [P, P], f32)
        ident16 = sb("ident16", [P, P], f16)
        row_id = sb("row_id", [P, max(CHUNKS)], f32)
        table = sb("table", [P, NCH, ROW], f32)
        table_parts = sb("table_parts", [P, NCH, SPLIT, ROW], bf16)
        onehot = sb("onehot", [P, NCH, PAIR], bf16)
        dense_sb = sb("dense_sb", [ND * DFOLD, BATCH // DFOLD], f32)
        dense_parts = sb("dense_parts", [ND * DFOLD, SPLIT, BATCH // DFOLD], bf16)
        dense_stack = sb("dense_stack", [NROWS, BATCH], bf16)
        wd_sb = sb("wd_sb", [D, ND], f32)
        wd_rep = sb("wd_rep", [D, SPLIT * SPLIT, ND], f32)
        take_rest = sb("take_rest", [NROWS, SPLIT - 1], f32)
        w1d_sb = sb("w1d_sb", [D, H1], f32)
        wdense = sb("wdense", [NROWS, H1 + 1], f32)
        wdense_parts = sb("wdense_parts", [NROWS, SPLIT - 1, H1 + 1], bf16)
        wdense_stack = sb("wdense_stack", [NROWS, H1 + 1], bf16)
        w1_sb = sb("w1_sb", [P, KB, H1], f32)
        w1_hi = sb("w1_hi", [P, KB, H1], f32r)
        w1_lo = sb("w1_lo", [P, KB, H1], f32r)
        w2_sb = sb("w2_sb", [P, M1, H2], f32)
        w2_hi = sb("w2_hi", [P, M1, H2], f32r)
        w2_lo = sb("w2_lo", [P, M1, H2], f32r)
        w3_sb = sb("w3_sb", [P, M2], f32)
        bias_sb = sb("bias_sb", [P, 1], f32)
        x = sb("x", [P, TILES, NF * ROW], f32)
        xt_hi = [sb(f"xt_hi{h}", [P, KB, BLOCK], f32r) for h in range(2)]
        xt_lo = [sb(f"xt_lo{h}", [P, KB, BLOCK], f32r) for h in range(2)]
        h1_hi = sb("h1_hi", [P, M1, BLOCK], f32r)
        h1_lo = sb("h1_lo", [P, M1, BLOCK], f32r)
        h2 = sb("h2", [P, M2, BLOCK], f32)
        h2_first = sb("h2_first", [P, BLOCK], f32)
        h2_w3 = sb("h2_w3", [P, BLOCK], f32)
        ones = sb("ones", [P, 1], f32)
        wide = sb("wide", [P, TILES], f32)
        cross = sb("cross", [P, NX, TILES], f32)
        wide_dense = sb("wide_dense", [P, TILES], f32)
        wide_bias = sb("wide_bias", [P, TILES], f32)
        wide_deep = sb("wide_deep", [P, TILES], f32)
        result = sb("result", [P, TILES], f32)

        look_ps = [pb(f"look_ps{k}", [P, BLOCK]) for k in range(LOOK_BANKS)]
        tr_ps = [pb(f"tr_ps{k}", [P, BLOCK]) for k in range(2)]
        mm_ps = [pb(f"mm_ps{k}", [P, BLOCK]) for k in range(2)]
        deep_ps = pb("deep_ps", [P, 2, TILES])

        index_loaded = sem("index_loaded")
        table_loaded = [sem(f"table_loaded{k}") for k in range(2)]
        dense_loaded = sem("dense_loaded")
        wd_loaded = sem("wd_loaded")
        wide_weight_loaded = sem("wide_weight_loaded")
        wd_replicated = sem("wd_replicated")
        take_rest_ready = sem("take_rest_ready")
        ones_ready = sem("ones_ready")
        w1_loaded = sem("w1_loaded")
        w2_loaded = sem("w2_loaded")
        w3_loaded = sem("w3_loaded")
        bias_loaded = sem("bias_loaded")
        zero_ready = sem("zero_ready")
        warm_up_ready = sem("warm_up_ready")
        ident_ready = sem("ident_ready")
        row_id_ready = sem("row_id_ready")
        vocab_ready = sem("vocab_ready")
        look_index_ready = sem("look_index_ready")
        gather_index_ready = sem("gather_index_ready")
        cross_index_ready = sem("cross_index_ready")
        index_spread = sem("index_spread")
        index_copied = sem("index_copied")
        wdense_done = sem("wdense_done")
        wdense_copied = sem("wdense_copied")
        table_a_rounded = sem("table_a_rounded")
        table_first_ready = sem("table_first_ready")
        table_rounded, table_rest, table_last = sem("table_rounded"), sem("table_rest"), sem("table_last")
        dense_rounded, dense_rest, dense_last = sem("dense_rounded"), sem("dense_rest"), sem("dense_last")
        wdense_rounded, wdense_rest, wdense_last = sem("wdense_rounded"), sem("wdense_rest"), sem("wdense_last")
        dense_stored = sem("dense_stored")
        dense_stacked = sem("dense_stacked")
        w1_high = sem("w1_high")
        w1_low = sem("w1_low")
        w2_high = sem("w2_high")
        w2_low = sem("w2_low")
        rows_gathered = [[sem(f"rows_gathered{b}_{k}") for k in range(NG // 2)] for b in range(BLOCKS)]
        cross_gathered = [sem(f"cross_gathered{c}") for c in range(NX)]
        onehot_ready = sem("onehot_ready")
        looked_up = sem("looked_up")
        rows_copied = sem("rows_copied")
        rows_summed = sem("rows_summed")
        turned = sem("turned")
        turned_high = sem("turned_high")
        turned_low = sem("turned_low")
        layer_done = sem("layer_done")
        layer1_low = sem("layer1_low")
        layer_high = sem("layer_high")
        dense_wide_done = sem("dense_wide_done")
        h2_used = sem("h2_used")
        deep_done = sem("deep_done")
        vector_step = sem("vector_step")
        result_ready = sem("result_ready")
        result_stored = sem("result_stored")

        CA = CHUNK0[GROUPS[0][-1]] + CHUNKS[GROUPS[0][-1]]
        table_a, table_a_parts = table[:, 0:CA], [table_parts[:, 0:CA, i, :] for i in range(SPLIT)]
        table_b, table_b_parts = table[:, CA:], [table_parts[:, CA:, i, :] for i in range(SPLIT)]
        dense_in, dense_in_parts = dense_sb[:], [dense_parts[:, i, :] for i in range(SPLIT)]

        def unit(n):
            return n // PT, n % PT

        def halves(b, m):
            return (0, 1) if (b, m) == (BLOCKS - 1, M2 - 1) else (None,)

        def samples(half):
            return slice(0, BLOCK) if half is None else slice(half * BLOCK // 2, (half + 1) * BLOCK // 2)

        def result_bank(n, half=None):
            return tr_ps[0] if half == 1 else mm_ps[n % 2]

        def merged(pair, n):
            return pair == 0 and n < MERGED

        def written(pair, n):
            kind = merged(pair, n)
            count = sum(merged(p, i) == kind for p in range(pair + 1) for i in range(UNITS if p < pair else n + 1))
            return (rows_copied if kind else rows_summed), count

        def turns_after(b, m):
            return [(), (0,), (1,), (), (2,), (3,)][m] if b + 1 < BLOCKS else ()

        def spread_bank(pair, n):
            return (look_ps + tr_ps + mm_ps + tr_ps)[n] if pair == 0 else look_ps[(UNITS + n) % LOOK_BANKS]

        block = ctx.enter_context(nc.Block())

        @block.sync
        def _(sp):
            sp.dma_start(idx_raw[:], index).then_inc(index_loaded, 16)
            sp.dma_start(table[:, 0:CA], small[:, 0:CA]).then_inc(table_loaded[0], 16)
            sp.dma_start(table[:, CA:], small[:, CA:]).then_inc(table_loaded[1], 16)
            sp.dma_start(wd_sb[:], wd_deep_t).then_inc(wd_loaded, 16)
            sp.dma_start(w1d_sb[:], w1[0:D, :]).then_inc(wd_loaded, 16)
            sp.dma_start(dense_sb[:], dense_t.rearrange("k (b n) -> (k b) n", b=DFOLD)).then_inc(dense_loaded, 16)
            sp.dma_start(w1_sb[:], w1[D:, :].rearrange("(k p) n -> p k n", p=P)).then_inc(w1_loaded, 16)
            sp.dma_start(w2_sb[:], w2.rearrange("(k p) n -> p k n", p=P)).then_inc(w2_loaded, 16)
            for r in range(0, NROWS, ND):
                sp.dma_start(wdense[r:r + ND, H1:H1 + 1], wd_wide).then_inc(wide_weight_loaded, 16)
            sp.dma_start(w3_sb[:], w3).then_inc(w3_loaded, 16)
            sp.dma_start(bias_sb[:], bias.to_broadcast([P, 1])).then_inc(bias_loaded, 16)
            sp.wait_ge(dense_last, 1)
            sp.dma_start(dense_dram.rearrange("s k (b n) -> (k b) s n", b=DFOLD), dense_parts[:])\
              .then_inc(dense_stored, 16)
            sp.wait_ge(dense_stored, 16)
            for b in range(SPLIT):
                r = b * SPLIT * ND
                sp.dma_start(dense_stack[r:r + SPLIT * ND, :], dense_dram.rearrange("s k n -> (s k) n"))\
                  .then_inc(dense_stacked, 16)
            sp.wait_ge(result_ready, 1)
            sp.dma_start(out, result[:]).then_inc(result_stored, 16)
            sp.wait_ge(result_stored, 16)

        @block.gpsimd
        def _(pool):
            nc.gpsimd.memset(zero[:], 0.0).then_inc(zero_ready, 1)
            nc.gpsimd.iota(row_id[:], pattern=[[P, max(CHUNKS)]], base=0, channel_multiplier=1,
                           allow_small_or_imprecise_dtypes=True).then_inc(row_id_ready, 1)
            pool.wait_ge(zero_ready, 1)
            for m in (ident16, ident):
                nc.gpsimd.affine_select(out=m[:], in_=zero[:], compare_op=ALU.not_equal, fill=1.0, base=0,
                                        pattern=[[-1, P]], channel_multiplier=1).then_inc(ident_ready, 1)
            nc.gpsimd.memset(ones[:], 1.0).then_inc(ones_ready, 1)
            pool.wait_ge(gather_index_ready, 1)
            for b in range(BLOCKS):
                for pair in range(NG // 2):
                    for t in range(b * BT, (b + 1) * BT):
                        for g in (2 * pair, 2 * pair + 1):
                            nc.gpsimd.indirect_dma_start(
                                out=x[:, t, g * ROW:(g + 1) * ROW], out_offset=None, in_=big[g],
                                in_offset=bass.IndirectOffsetOnAxis(ap=idx_gather[:, g, t:t + 1], axis=0),
                            ).then_inc(rows_gathered[b][pair], 16)
            pool.wait_ge(cross_index_ready, 1)
            for c in range(NX):
                for t in range(TILES):
                    nc.gpsimd.indirect_dma_start(
                        out=cross[:, c, t:t + 1], out_offset=None, in_=wc[c],
                        in_offset=bass.IndirectOffsetOnAxis(ap=idx_cross[:, c, t:t + 1], axis=0),
                    ).then_inc(cross_gathered[c], 16)

        @block.scalar
        def _(act):
            def copy_spread(pair, n):
                i, h = n // 2, n % 2
                act.wait_ge(index_spread, pair * SPREADS + n + 1)
                if pair and h == 0:
                    act.wait_ge(onehot_ready, BUILT[i])
                nc.scalar.copy(idx_bc[:, i, h * BLOCK:(h + 1) * BLOCK], spread_bank(pair, n)[:])\
                    .then_inc(index_copied, 1)

            def turned_hi(b, q):
                n = b * KB + q
                act.wait_ge(turned, n + 1)
                nc.scalar.copy(xt_hi[b % 2][:, TURN_ORDER[q], :], tr_ps[n % 2][:]).then_inc(turned_high, 1)

            def relu(n, dst, half=None):
                act.wait_ge(layer_done, n + 1 + (half == 1))
                s = samples(half)
                nc.scalar.activation(dst[:, s], result_bank(n, half)[:, s], ACT.Relu).then_inc(layer_high, 1)

            def weight_high(q):
                g = TURN_ORDER[q]
                nc.scalar.copy(w1_hi[:, g, :], w1_sb[:, g, :]).then_inc(w1_high, 1)

            def copy_rows(n):
                k, t = unit(n)
                lo, hi = (NG + GROUPS[k][0]) * ROW, (NG + GROUPS[k][-1] + 1) * ROW
                act.wait_ge(looked_up, n + 1)
                nc.scalar.copy(x[:, t, lo:hi], look_ps[n % LOOK_BANKS][:, 0:hi - lo]).then_inc(rows_copied, 1)

            act.wait_ge(table_loaded[0], 16)
            nc.scalar.copy(table_a_parts[0], table_a).then_inc(table_a_rounded, 1)
            for n in range(4):
                copy_spread(0, n)
            act.wait_ge(table_loaded[1], 16)
            nc.scalar.copy(table_b_parts[0], table_b).then_inc(table_rounded, 1)
            for n in range(4, SPREADS):
                copy_spread(0, n)
            act.wait_ge(wd_loaded, 32)
            nc.scalar.copy(wd_rep[:], wd_sb[:].unsqueeze(1).to_broadcast([D, SPLIT * SPLIT, ND]))\
                .then_inc(wd_replicated, 1)
            act.wait_ge(table_rest, 1)
            nc.scalar.copy(table_b_parts[1], table_b).then_inc(table_rounded, 1)
            copy_rows(0)
            copy_rows(1)
            act.wait_ge(dense_loaded, 16)
            nc.scalar.copy(dense_in_parts[0], dense_in).then_inc(dense_rounded, 1)
            act.wait_ge(w1_loaded, 16)
            weight_high(0)
            copy_rows(2)
            copy_rows(3)
            act.wait_ge(dense_rest, 1)
            nc.scalar.copy(dense_in_parts[1], dense_in).then_inc(dense_rounded, 1)
            copy_rows(4)
            copy_rows(5)
            weight_high(1)
            act.wait_ge(wdense_done, 1)
            nc.scalar.copy(wdense[:, 0:H1], mm_ps[1][0:NROWS, :]).then_inc(wdense_copied, 1)
            act.wait_ge(wdense_copied, 1)
            act.wait_ge(wide_weight_loaded, 16 * SPLIT * SPLIT)
            copy_rows(6)
            copy_rows(7)
            nc.scalar.copy(wdense_parts[:, 0, :], wdense[:]).then_inc(wdense_rounded, 1)
            for n in range(PT, MERGED):
                copy_rows(n)
            act.wait_ge(wdense_rest, 1)
            nc.scalar.copy(wdense_parts[:, 1, :], wdense[:]).then_inc(wdense_rounded, 1)
            turned_hi(0, 0)
            weight_high(2)
            turned_hi(0, 1)
            weight_high(3)
            copy_spread(1, 0)
            turned_hi(0, 2)
            copy_spread(1, 1)
            copy_spread(1, 2)
            act.wait_ge(w2_loaded, 16)
            nc.scalar.copy(w2_hi[:], w2_sb[:]).then_inc(w2_high, 1)
            turned_hi(0, 3)
            copy_spread(1, 3)
            copy_spread(1, 4)
            for b in range(BLOCKS):
                for m in range(M1):
                    n = b * TURNS + m
                    relu(n, h1_hi[:, m, :])
                    for k in slot(SPREAD_SLOTS, n):
                        copy_spread(1, k)
                    for g in turns_after(b, m):
                        turned_hi(b + 1, g)
                for m in range(M2):
                    if b > 0:
                        act.wait_ge(h2_used, (b - 1) * M2 + m + 1)
                    for half in halves(b, m):
                        relu(b * TURNS + M1 + m, h2[:, m, :], half)
                    for g in turns_after(b, M1 + m):
                        turned_hi(b + 1, g)

        @block.vector
        def _(dve):
            steps = [0]

            def step(ins):
                steps[0] += 1
                ins.then_inc(vector_step, 1)
                dve.wait_ge(vector_step, steps[0])

            nc.vector.memset(zero16[:], 0.0).then_inc(warm_up_ready, 1)
            sizes = [VOCABS[f] for f in FIELDS] + [VOCABS[a] * VOCABS[b] for a, b in CROSSES]
            for k, v in enumerate(sizes):
                nc.vector.memset(vocab[:, k, :], float(v)).then_inc(vocab_ready, 1)
                nc.vector.memset(vocab_last[:, k, :], float(v - 1)).then_inc(vocab_ready, 1)

            def index_sum(src, lo, hi):
                step(nc.vector.scalar_tensor_tensor(out=idx_wrap[:, lo:hi], in0=src, scalar=0.0,
                                                    in1=vocab[:, lo:hi], op0=ALU.is_lt, op1=ALU.mult))
                step(nc.vector.tensor_tensor(idx_sum[:, lo:hi], idx_wrap[:, lo:hi], src, ALU.add))

            def index_clip(dst, lo, hi, ready):
                nc.vector.scalar_tensor_tensor(out=dst[:], in0=idx_sum[:, lo:hi], scalar=0.0,
                                               in1=vocab_last[:, lo:hi], op0=ALU.max, op1=ALU.min).then_inc(ready, 1)

            dve.wait_ge(index_loaded, 16)
            dve.wait_ge(vocab_ready, 2 * len(sizes))
            index_sum(idx_raw[:], 0, NF)
            index_clip(idx_look, NG, NF, look_index_ready)
            index_clip(idx_gather, 0, NG, gather_index_ready)

            def build_onehot(pair, chunks):
                for c in chunks:
                    i = max(k for k in range(NL) if CHUNK0[k] <= c)
                    if c == CHUNK0[i]:
                        dve.wait_ge(index_copied, pair * SPREADS + 2 * i + 2)
                    nc.vector.tensor_scalar(
                        onehot[:, c, :], idx_bc[:, i, :], row_id[:, c - CHUNK0[i]:c - CHUNK0[i] + 1],
                        None, ALU.is_equal).then_inc(onehot_ready, 1)

            def weight_low(dst, src, hi, ready, count, done):
                dve.wait_ge(ready, count)
                nc.vector.tensor_tensor(dst, src, hi.bitcast(f32), ALU.subtract).then_inc(done, 1)

            def w1_low_part(q):
                g = TURN_ORDER[q]
                weight_low(w1_lo[:, g, :], w1_sb[:, g, :], w1_hi[:, g, :], w1_high, q + 1, w1_low)

            def sum_parts(pair, n):
                k, t = unit(n)
                group = GROUPS[k]
                dve.wait_ge(looked_up, pair * UNITS + n + 1)
                nc.vector.tensor_reduce(
                    x[:, pair * PT + t, (NG + group[0]) * ROW:(NG + group[-1] + 1) * ROW]
                    .rearrange("p (f n) -> p f n", n=ROW),
                    look_ps[n % LOOK_BANKS][:, 0:len(group) * SPLIT * ROW]
                    .rearrange("p (f c n) -> p f n c", c=SPLIT, n=ROW), AX.X, ALU.add,
                ).then_inc(rows_summed, 1)

            def turned_lo(b, q):
                n, g = b * KB + q, TURN_ORDER[q]
                dve.wait_ge(turned_high, n + 1)
                nc.vector.tensor_tensor(xt_lo[b % 2][:, g, :], tr_ps[n % 2][:], xt_hi[b % 2][:, g, :].bitcast(f32),
                                        ALU.subtract).then_inc(turned_low, 1)

            def relu_lo(b, m):
                n = b * TURNS + m
                dve.wait_ge(layer_high, n + 1)
                nc.vector.scalar_tensor_tensor(out=h1_lo[:, m, :], in0=mm_ps[n % 2][:], scalar=0.0,
                                               in1=h1_hi[:, m, :].bitcast(f32), op0=ALU.max,
                                               op1=ALU.subtract).then_inc(layer1_low, 1)

            def beside(n):
                build, sums = list(slot(ONEHOT_SLOTS, n)), list(slot(LOOK_SLOTS, n))
                for k in range(max(len(build), len(sums))):
                    for q in sums[k:k + 1]:
                        sum_parts(1, q)
                    build_onehot(1, build[k:k + 1])

            def weigh(b):
                if b == 0:
                    dve.wait_ge(w3_loaded, 16)
                dve.wait_ge(layer_high, b * TURNS + M1 + 1)
                nc.vector.tensor_scalar(h2_first[:], h2[:, 0, :], w3_sb[:, 0:1], None, ALU.mult).then_inc(h2_used, 1)
                dve.wait_ge(h2_used, b * M2 + 1)
                if b > 0:
                    dve.wait_ge(deep_done, b)
                for half in halves(b, 1):
                    dve.wait_ge(layer_high, b * TURNS + M1 + 2 + (half == 1))
                    s = samples(half)
                    nc.vector.scalar_tensor_tensor(out=h2_w3[:, s], in0=h2[:, 1, s], scalar=w3_sb[:, 1:2],
                                                   in1=h2_first[:, s], op0=ALU.mult, op1=ALU.add)\
                        .then_inc(h2_used, 1)

            dve.wait_ge(table_a_rounded, 1)
            step(nc.vector.tensor_tensor(table_a, table_a, table_a_parts[0], ALU.subtract))
            step(nc.vector.tensor_copy(table_a_parts[1], table_a))
            nc.vector.tensor_tensor(table_a_parts[2], table_a, table_a_parts[1], ALU.subtract)\
                .then_inc(table_first_ready, 1)

            dve.wait_ge(row_id_ready, 1)
            build_onehot(0, range(0, CA))
            dve.wait_ge(table_rounded, 1)
            nc.vector.tensor_tensor(table_b, table_b, table_b_parts[0], ALU.subtract).then_inc(table_rest, 1)
            build_onehot(0, range(CA, NCH))
            for part in range(1, SPLIT):
                nc.vector.tensor_scalar(take_rest[:, part - 1:part], row_id[0:NROWS, 0:1], float(part * SPLIT * ND), -1.0,
                                        ALU.is_ge, ALU.mult).then_inc(take_rest_ready, 1)
            dve.wait_ge(table_rounded, 2)
            dve.wait_ge(table_rest, 1)
            nc.vector.tensor_tensor(table_b_parts[2], table_b, table_b_parts[1], ALU.subtract).then_inc(table_last, 1)
            dve.wait_ge(dense_rounded, 1)
            nc.vector.tensor_tensor(dense_in, dense_in, dense_in_parts[0], ALU.subtract).then_inc(dense_rest, 1)
            w1_low_part(0)
            dve.wait_ge(dense_rounded, 2)
            dve.wait_ge(dense_rest, 1)
            nc.vector.tensor_tensor(dense_in_parts[2], dense_in, dense_in_parts[1], ALU.subtract).then_inc(dense_last, 1)
            w1_low_part(1)
            for n in range(MERGED, UNITS):
                sum_parts(0, n)
                if n == WDENSE_AFTER[0]:
                    dve.wait_ge(wdense_rounded, 1)
                    dve.wait_ge(take_rest_ready, SPLIT - 1)
                    nc.vector.scalar_tensor_tensor(out=wdense[:], in0=wdense_parts[:, 0, :],
                                                   scalar=take_rest[:, 0:1], in1=wdense[:],
                                                   op0=ALU.mult, op1=ALU.add).then_inc(wdense_rest, 1)
                if n == WDENSE_AFTER[1]:
                    dve.wait_ge(wdense_rounded, 2)
                    dve.wait_ge(wdense_rest, 1)
                    nc.vector.scalar_tensor_tensor(out=wdense_stack[:], in0=wdense_parts[:, 1, :],
                                                   scalar=take_rest[:, 1:2], in1=wdense[:],
                                                   op0=ALU.mult, op1=ALU.add).then_inc(wdense_last, 1)
                if n == FIRST_TURN_AFTER + 1:
                    turned_lo(0, 0)
            turned_lo(0, 1)
            w1_low_part(2)
            turned_lo(0, 2)
            w1_low_part(3)
            turned_lo(0, 3)
            for c, (a, b) in enumerate(CROSSES):
                ins = nc.vector.scalar_tensor_tensor(
                    out=idx_pair[:, c, :], in0=idx_raw[:, FIELDS.index(a), :], scalar=float(VOCABS[b]),
                    in1=idx_raw[:, FIELDS.index(b), :], op0=ALU.mult, op1=ALU.add)
            step(ins)
            index_sum(idx_pair[:], NF, NF + NX)
            index_clip(idx_cross, NF, NF + NX, cross_index_ready)
            build_onehot(1, ONEHOT_FIRST)
            for b in range(BLOCKS):
                for m in range(M1):
                    n = b * TURNS + m
                    relu_lo(b, m)
                    beside(n)
                    if n == 1:
                        weight_low(w2_lo[:], w2_sb[:], w2_hi[:], w2_high, 1, w2_low)
                    if m == 0 and b > 0:
                        weigh(b - 1)
                    for g in turns_after(b, m):
                        turned_lo(b + 1, g)
                for m in range(M2):
                    beside(b * TURNS + M1 + m)
                    for g in turns_after(b, M1 + m):
                        turned_lo(b + 1, g)
            for b in range(BLOCKS):
                for k in range(NG // 2):
                    dve.wait_ge(rows_gathered[b][k], 16 * 2 * BT)
            for pair, n in ((0, MERGED - 1), (1, UNITS - 1)):
                dve.wait_ge(*written(pair, n))
            step(nc.vector.tensor_reduce(
                wide[:], x[:].rearrange("p t (g n) -> p t g n", n=2 * ROW)[:, :, :, 0:2 * ROW:2 * ROW - 1],
                AX.XY, ALU.add))
            dve.wait_ge(dense_wide_done, 1)
            step(nc.vector.tensor_tensor(wide_dense[:], wide[:], deep_ps[:, 1, :], ALU.add))
            dve.wait_ge(bias_loaded, 16)
            dve.wait_ge(cross_gathered[0], 16 * TILES)
            step(nc.vector.scalar_tensor_tensor(out=wide_bias[:], in0=cross[:, 0, :], scalar=bias_sb[:, 0:1],
                                                in1=wide_dense[:], op0=ALU.add, op1=ALU.add))
            weigh(BLOCKS - 1)
            dve.wait_ge(deep_done, BLOCKS + 1)
            step(nc.vector.tensor_tensor(wide_deep[:], wide_bias[:], deep_ps[:, 0, :], ALU.add))
            dve.wait_ge(cross_gathered[1], 16 * TILES)
            nc.vector.tensor_tensor(result[:], wide_deep[:], cross[:, 1, :], ALU.add).then_inc(result_ready, 1)

        @block.tensor
        def _(pe):
            def spread_index(pair, n):
                i, h = n // 2, n % 2
                bank = spread_bank(pair, n)
                if pair == 0:
                    before = [k for k in range(n) if spread_bank(0, k) is bank]
                    if before:
                        pe.wait_ge(index_copied, before[-1] + 1)
                elif n >= LOOK_BANKS:
                    pe.wait_ge(index_copied, pair * SPREADS + n - LOOK_BANKS + 1)
                else:
                    pe.wait_ge(*written(0, UNITS - LOOK_BANKS + n))
                for s in range(BT):
                    t = pair * PT + h * BT + s
                    last = nc.tensor.matmul(bank[:, s * P:(s + 1) * P],
                                            idx_look[:, i, t:t + 1].to_broadcast([P, P]), ident16[:],
                                            start=True, stop=True)
                last.then_inc(index_spread, 1)

            def look_up(pair, n):
                k, t = unit(n)
                if n == PT and pair == 0:
                    pe.wait_ge(table_last, 1)
                if n >= LOOK_BANKS:
                    pe.wait_ge(*written(pair, n - LOOK_BANKS))
                else:
                    pe.wait_ge(index_copied, n + 1 if pair == 0 else 2 * SPREADS)
                group = GROUPS[k]
                for i in group:
                    if t == 0:
                        pe.wait_ge(onehot_ready, pair * NCH + BUILT[i])
                    rows = table_parts[:, CHUNK0[i]:CHUNK0[i] + CHUNKS[i], :, :]
                    if merged(pair, n):
                        at = (i - group[0]) * ROW
                        passes = [(c, rows[:, c, p, :]) for c in range(CHUNKS[i]) for p in range(SPLIT)]
                    else:
                        at = (i - group[0]) * SPLIT * ROW
                        passes = [(c, rows[:, c, :, :].rearrange("p c n -> p (c n)")) for c in range(CHUNKS[i])]
                    for q, (c, part) in enumerate(passes):
                        last = nc.tensor.matmul(look_ps[n % LOOK_BANKS][:, at:at + part.shape[-1]],
                                                onehot[:, CHUNK0[i] + c, t * P:(t + 1) * P], part,
                                                start=q == 0, stop=q == len(passes) - 1)
                last.then_inc(looked_up, 1)

            def turn(b, q):
                n, g = b * KB + q, TURN_ORDER[q]
                if g < NG // 2:
                    pe.wait_ge(rows_gathered[b][g], 16 * 2 * BT)
                else:
                    pe.wait_ge(*written(b // 2, (g - NG // 2 + 1) * PT - 1))
                if n >= 2:
                    pe.wait_ge(turned_low, n - 1)
                else:
                    pe.wait_ge(index_copied, SPREADS)
                for s in range(BT):
                    last = nc.tensor.transpose(tr_ps[n % 2][:, s * P:(s + 1) * P],
                                               x[:, b * BT + s, 2 * g * ROW + 1:2 * g * ROW + 1 + 2 * D], ident[:])
                last.then_inc(turned, 1)

            def wait_bank(n):
                if n >= 2:
                    pe.wait_ge(layer_high, n - 1)
                    b, m = (n - 2) // TURNS, (n - 2) % TURNS
                    if m < M1:
                        pe.wait_ge(layer1_low, b * M1 + m + 1)

            def product(dst, w_hi, w_lo, a_hi, a_lo, start, stop):
                nc.tensor.matmul(dst, w_hi, a_hi, start=start, stop=False)
                nc.tensor.matmul(dst, w_hi, a_lo, start=False, stop=False)
                return nc.tensor.matmul(dst, w_lo, a_hi, start=False, stop=stop)

            def layer1(b, m, blocks=range(KB)):
                n = b * TURNS + m
                if 0 in blocks:
                    wait_bank(n)
                    nc.tensor.matmul(mm_ps[n % 2][:], wdense_stack[:, m * P:(m + 1) * P],
                                     dense_stack[:, b * BLOCK:(b + 1) * BLOCK], start=True, stop=False)
                c = slice(m * P, (m + 1) * P)
                for q in blocks:
                    g = TURN_ORDER[q]
                    if b == 0 and m == 0:
                        pe.wait_ge(w1_low, q + 1)
                    if m == 0:
                        pe.wait_ge(turned_low, b * KB + q + 1)
                    last = product(mm_ps[n % 2][:], w1_hi[:, g, c], w1_lo[:, g, c], xt_hi[b % 2][:, g, :],
                                   xt_lo[b % 2][:, g, :], False, q == KB - 1)
                if KB - 1 in blocks:
                    last.then_inc(layer_done, 1)

            def layer2(b, m, half=None):
                n = b * TURNS + M1 + m
                if half != 1:
                    wait_bank(n)
                c, s = slice(m * P, (m + 1) * P), samples(half)
                bank = result_bank(n, half)
                for k in range(M1):
                    if m == 0:
                        pe.wait_ge(layer1_low, b * M1 + k + 1)
                    last = product(bank[:, s], w2_hi[:, k, c], w2_lo[:, k, c], h1_hi[:, k, s],
                                   h1_lo[:, k, s], k == 0, k == M1 - 1)
                last.then_inc(layer_done, 1)

            def layer3(b, half=None):
                pe.wait_ge(h2_used, (b + 1) * M2 + (half == 1))
                if b == 0:
                    pe.wait_ge(ones_ready, 1)
                s = samples(half)
                for at in range(s.start, s.stop, P):
                    t = b * BT + at // P
                    last = nc.tensor.matmul(deep_ps[:, 0, t:t + 1], h2_w3[:, at:at + P], ones[:],
                                            start=True, stop=True)
                last.then_inc(deep_done, 1)

            pe.wait_ge(warm_up_ready, 1)
            for _ in range(WARM_UP):
                nc.tensor.matmul(mm_ps[1][:], zero16[:, 0:P], zero16[:], start=True, stop=True)
            pe.wait_ge(ident_ready, 2)
            pe.wait_ge(look_index_ready, 1)
            for n in range(SPREADS):
                spread_index(0, n)
            pe.wait_ge(table_first_ready, 1)
            for n in range(UNITS):
                look_up(0, n)
                if n == FIRST_TURN_AFTER:
                    turn(0, 0)
                if n == UNITS - 1:
                    turn(0, 1)
                if n == 1:
                    pe.wait_ge(wd_replicated, 1)
                    pe.wait_ge(index_copied, 7)
                    nc.tensor.matmul(mm_ps[1][0:NROWS, :], wd_rep[:].rearrange("p r k -> p (r k)"), w1d_sb[:],
                                     start=True, stop=True).then_inc(wdense_done, 1)
            pe.wait_ge(wdense_last, 1)
            pe.wait_ge(dense_stacked, 16 * SPLIT)
            layer1(0, 0, range(0, 1))
            spread_index(1, 0)
            turn(0, 2)
            layer1(0, 1, range(0, 1))
            spread_index(1, 1)
            layer1(0, 0, range(1, 2))
            spread_index(1, 2)
            layer1(0, 1, range(1, 2))
            for t in range(TILES):
                last = nc.tensor.matmul(deep_ps[:, 1, t:t + 1], dense_stack[:, t * P:(t + 1) * P],
                                        wdense_stack[:, H1:H1 + 1], start=True, stop=True)
            last.then_inc(dense_wide_done, 1)
            turn(0, 3)
            layer1(0, 0, range(2, 3))
            spread_index(1, 3)
            spread_index(1, 4)
            layer1(0, 1, range(2, 3))
            for b in range(BLOCKS):
                for m in range(M1):
                    n = b * TURNS + m
                    layer1(b, m, range(KB - 1, KB) if n < 2 else range(KB))
                    if m == 1 and b > 0:
                        layer3(b - 1)
                    for k in slot(SPREAD_SLOTS, n):
                        spread_index(1, k)
                    for k in slot(LOOK_SLOTS, n):
                        look_up(1, k)
                    for g in turns_after(b, m):
                        turn(b + 1, g)
                if b == 0:
                    pe.wait_ge(w2_low, 1)
                for m in range(M2):
                    for half in halves(b, m):
                        layer2(b, m, half)
                    for k in slot(LOOK_SLOTS, b * TURNS + M1 + m):
                        look_up(1, k)
                    for q in turns_after(b, M1 + m):
                        turn(b + 1, q)
            for half in range(2):
                layer3(BLOCKS - 1, half)


def kernel(**inputs):
    import concourse.bacc as bacc
    from concourse.bass_utils import run_bass_kernel_spmd

    a = {k: np.ascontiguousarray(v) for k, v in inputs.items()}
    table = {}
    for k, f in enumerate(FIELDS):
        row = [a[f"L0_rec_w{f}"], a[f"L0_rec_E{f}"]]
        table[f] = np.concatenate(row if k % 2 == 0 else row[::-1], axis=1)
    index = np.stack([a[f"r_s{f}"].reshape(TILES, P) for f in FIELDS])
    small = np.concatenate([np.pad(table[f], ((0, -VOCABS[f] % P), (0, 0))) for f in LOOKED_UP])
    w1 = a["L0_rec_W1"].reshape(1 + NF, D, H1)[[0] + [1 + f for f in FIELDS]].reshape(-1, H1)
    arrays = {
        "index": index.transpose(2, 0, 1),
        "dense_t": a["r_dense"].T,
        "small": small.reshape(NCH, P, ROW).transpose(1, 0, 2),
        "wd_deep_t": a["L0_rec_Wd_deep"].T,
        "wd_wide": a["L0_rec_Wd_wide"],
        "w1": w1,
        "w2": a["L0_rec_W2"],
        "w3": a["L0_rec_W3"].reshape(M2, P).T,
        "bias": a["L0_rec_bias"],
    }
    for f in GATHERED:
        arrays[f"rows{f}"] = table[f]
    for c in range(NX):
        arrays[f"wc{c}"] = a[f"L0_rec_wc{c}"]
    arrays = {f"in_{k}_dram": np.ascontiguousarray(v) for k, v in arrays.items()}

    nc = bacc.Bacc("TRN2", target_bir_lowering=False, num_devices=1)
    ap = {k: nc.dram_tensor(k, v.shape, mybir.dt.from_np(v.dtype), kind="ExternalInput").ap()
          for k, v in arrays.items()}
    out = nc.dram_tensor("out_dram", (P, TILES), mybir.dt.float32, kind="ExternalOutput").ap()

    def one(name):
        return ap[f"in_{name}_dram"]

    program(nc, one("index"), one("dense_t"), [one(f"rows{f}") for f in GATHERED], one("small"),
            [one(f"wc{c}") for c in range(NX)], one("wd_deep_t"), one("wd_wide"), one("w1"), one("w2"),
            one("w3"), one("bias"), out)
    r = run_bass_kernel_spmd(nc, [arrays], core_ids=[0])
    return np.ascontiguousarray(r.results[0]["out_dram"].T).reshape(BATCH, 1)
```
